# Optimizing a Trainium2 kernel written in Bass

```python
import numpy as np
import jax
import jax.numpy as jnp

def _softmax(x, axis=-1):
    return jax.nn.softmax(x, axis=axis)
def _gelu(x):
    return jax.nn.gelu(x, approximate=True)
def _silu(x):
    return jax.nn.silu(x)
def _sigmoid(x):
    return jax.nn.sigmoid(x)
def _layernorm(x, axis=-1, eps=1e-5):
    m = jnp.mean(x, axis=axis, keepdims=True)
    v = jnp.var(x, axis=axis, keepdims=True)
    return (x - m) / jnp.sqrt(v + eps)
def _scatter_add(tgt, idx, src, axis=0):
    return tgt.at[idx].add(src)
def _segment_sum(src, seg, n):
    return jax.ops.segment_sum(src, seg, n)

kernel_name = 'mk_adj_resnorm_d4_adj_64_f8dcdc'

def setup_inputs(seed: int = 0):
    np.random.seed(seed)
    _w = jnp.asarray
    def _rec_inputs():
        import jax
        import jax.numpy as jnp
        _gk = jax.random.key(seed)
        x = -0.000929 + 1 * jax.random.normal(jax.random.fold_in(_gk, 1), (16, 1024, 64), jnp.float32)
        _w = (1.0 + jnp.arange(1024, dtype=jnp.float32)) ** -0.5
        _w = _w / _w.mean()
        _pij = jnp.clip(0.015625 * _w[:, None] * _w[None, :], 0.0, 1.0)
        _a = jax.random.uniform(jax.random.fold_in(_gk, 2), (1024, 1024)) < _pij
        adj = _a.astype(jnp.int32)
        return x, adj
    x, adj = _rec_inputs()
    def _L0_gnn_setup():
        import jax, jax.numpy as jnp
        import numpy as np
        ALPHA = 0.2
        key = jax.random.key(seed)
        k1, k2, k3, k4 = jax.random.split(key, 4)
        B, N, Fin, Fout = (4, 4096, 64, 64)
        h = jax.random.normal(k1, (B, N, Fin), dtype=jnp.float32)
        W = jax.random.normal(k2, (Fin, Fout), dtype=jnp.float32) * (1.414 / np.sqrt(Fin))
        a = jax.random.normal(k3, (2 * Fout, 1), dtype=jnp.float32) * 0.1
        adj = jax.random.randint(k4, (N, N), 0, 2, dtype=jnp.int32)
        return {'h': h, 'W': W, 'a': a, 'adj': adj}
    _L0_gnn_all = _L0_gnn_setup()
    _L0_gnn_in = {k: v for k, v in _L0_gnn_all.items() if k in ('W', 'a', )}
    del _L0_gnn_all

    def _L1_gnn_setup():
        import jax, jax.numpy as jnp
        import numpy as np
        INV_SQRT2 = 0.7071067811865476
        key = jax.random.key(seed)
        k = jax.random.split(key, 6)
        batch, node, dim = (4, 512, 64)
        x = jax.random.normal(k[0], (batch, node, dim), dtype=jnp.float32)
        w0 = jax.random.normal(k[1], (1, 1), dtype=jnp.float32)
        b0 = jax.random.normal(k[2], (1,), dtype=jnp.float32)
        wa = jax.random.normal(k[3], (dim,), dtype=jnp.float32)
        ba = jax.random.normal(k[4], (dim,), dtype=jnp.float32)
        adj = jax.random.randint(k[5], (node, node), 0, 2, dtype=jnp.int32)
        return {'x': x, 'w0': w0, 'b0': b0, 'wa': wa, 'ba': ba, 'adj': adj}
    _L1_gnn_all = _L1_gnn_setup()
    _L1_gnn_in = {k: v for k, v in _L1_gnn_all.items() if k in ('w0', 'b0', 'wa', 'ba', )}
    del _L1_gnn_all

    def _L2_gnn_setup():
        import jax, jax.numpy as jnp
        import numpy as np
        ALPHA = 0.2
        NEG_INF = -9000000000000000.0
        key = jax.random.key(seed)
        k1, k2, k3, k4 = jax.random.split(key, 4)
        B, N, Fin, Fout = (8, 2048, 64, 64)
        inp = jax.random.normal(k1, (B, N, Fin), dtype=jnp.float32)
        adj = jax.random.randint(k2, (N, N), 0, 2, dtype=jnp.int32)
        W = jax.random.normal(k3, (Fin, Fout), dtype=jnp.float32) * np.sqrt(2.0 / Fout)
        a = jax.random.normal(k4, (2 * Fout, 1), dtype=jnp.float32) * np.sqrt(2.0 / (2 * Fout + 1))
        return {'input': inp, 'adj': adj, 'W': W, 'a': a}
    _L2_gnn_all = _L2_gnn_setup()
    _L2_gnn_in = {k: v for k, v in _L2_gnn_all.items() if k in ('W', 'a', )}
    del _L2_gnn_all

    def _L3_gnn_setup():
        import jax, jax.numpy as jnp
        import numpy as np
        NEG = -1e+16
        LN_EPS = 1e-05

        def _gat_layer(h, mask, b):
            scores = jnp.einsum('...nd,...md->...nm', h, h)
            scores = jnp.where(mask, scores, NEG)
            attn = jax.nn.softmax(scores, axis=-1)
            return jnp.einsum('...nm,...md->...nd', attn, h) + b
        key = jax.random.key(seed)
        ks = jax.random.split(key, 6)
        B, N, C, H, D = (8, 2048, 64, 4, 64)
        x = jax.random.normal(ks[0], (B, N, C), dtype=jnp.float32)
        graph = jax.random.randint(ks[1], (N, N), 0, 2, dtype=jnp.int32)
        bnd_h = float(np.sqrt(6.0 / (C + D)))
        Wh = jax.random.uniform(ks[2], (H, D, C), jnp.float32, -bnd_h, bnd_h)
        bh = jnp.zeros((H, D), jnp.float32)
        bnd_o = float(np.sqrt(6.0 / (H * D + D)))
        Wo = jax.random.uniform(ks[3], (D, H * D), jnp.float32, -bnd_o, bnd_o)
        bo = jnp.zeros((D,), jnp.float32)
        gamma = jnp.ones((D,), jnp.float32)
        beta = jnp.zeros((D,), jnp.float32)
        return {'x': x, 'graph': graph, 'Wh': Wh, 'bh': bh, 'Wo': Wo, 'bo': bo, 'gamma': gamma, 'beta': beta}
    _L3_gnn_all = _L3_gnn_setup()
    _L3_gnn_in = {k: v for k, v in _L3_gnn_all.items() if k in ('Wh', 'bh', 'Wo', 'bo', 'gamma', 'beta', )}
    del _L3_gnn_all

    return {
        "x": x,
        "adj": adj,
        "L0_gnn_W": _L0_gnn_in["W"],
        "L0_gnn_a": _L0_gnn_in["a"],
        "L1_gnn_w0": _L1_gnn_in["w0"],
        "L1_gnn_b0": _L1_gnn_in["b0"],
        "L1_gnn_wa": _L1_gnn_in["wa"],
        "L1_gnn_ba": _L1_gnn_in["ba"],
        "L2_gnn_W": _L2_gnn_in["W"],
        "L2_gnn_a": _L2_gnn_in["a"],
        "L3_gnn_Wh": _L3_gnn_in["Wh"],
        "L3_gnn_bh": _L3_gnn_in["bh"],
        "L3_gnn_Wo": _L3_gnn_in["Wo"],
        "L3_gnn_bo": _L3_gnn_in["bo"],
        "L3_gnn_gamma": _L3_gnn_in["gamma"],
        "L3_gnn_beta": _L3_gnn_in["beta"],
    }

def reference(x, adj, L0_gnn_W, L0_gnn_a, L1_gnn_w0, L1_gnn_b0, L1_gnn_wa, L1_gnn_ba, L2_gnn_W, L2_gnn_a, L3_gnn_Wh, L3_gnn_bh, L3_gnn_Wo, L3_gnn_bo, L3_gnn_gamma, L3_gnn_beta):
    import jax
    import jax.numpy as jnp
    def _L0_gnn_ref(h, W, a, adj):
        import jax, jax.numpy as jnp
        import numpy as np
        ALPHA = 0.2
        Fout = W.shape[1]
        Wh = jnp.einsum('bni,io->bno', h, W)
        a1 = a[:Fout, 0]
        a2 = a[Fout:, 0]
        s1 = Wh @ a1
        s2 = Wh @ a2
        e = jax.nn.leaky_relu(s1[:, :, None] + s2[:, None, :], negative_slope=ALPHA)
        mask = jnp.where(adj == 0, jnp.float32(-1000000000.0), jnp.float32(0.0))
        e = e + mask[None, :, :]
        attention = jax.nn.softmax(e, axis=2)
        h_prime = jnp.einsum('bnm,bmo->bno', attention, Wh)
        return jax.nn.elu(h_prime)

    def _L1_gnn_ref(x, w0, b0, wa, ba, adj):
        import jax, jax.numpy as jnp
        import numpy as np
        INV_SQRT2 = 0.7071067811865476
        feat = jax.nn.softplus(x * (INV_SQRT2 * w0[0, 0]) + b0[0])
        scores = feat * wa + ba
        mask = adj > 0
        logits = scores[:, None, :, :] * mask[None, :, :, None].astype(scores.dtype)
        logits = jnp.where(mask[None, :, :, None], logits, jnp.float32(-1000000000.0))
        attn = jax.nn.softmax(logits, axis=2)
        out = jnp.einsum('bijd,bjd->bid', attn, feat)
        return out

    def _L2_gnn_ref(input, adj, W, a):
        import jax, jax.numpy as jnp
        import numpy as np
        ALPHA = 0.2
        NEG_INF = -9000000000000000.0
        h = jnp.matmul(input, W)
        Fout = W.shape[1]
        a1 = a[:Fout, 0]
        a2 = a[Fout:, 0]
        s1 = jnp.einsum('bnf,f->bn', h, a1)
        s2 = jnp.einsum('bnf,f->bn', h, a2)
        e = s1[:, :, None] + s2[:, None, :]
        e = jnp.where(e > 0, e, ALPHA * e)
        masked = jnp.where(adj[None, :, :] > 0, e, NEG_INF)
        attention = jax.nn.softmax(masked, axis=-1)
        h_prime = jnp.matmul(attention, h)
        return jax.nn.elu(h_prime)

    def _L3_gnn_ref(x, graph, Wh, bh, Wo, bo, gamma, beta):
        import jax, jax.numpy as jnp
        import numpy as np
        NEG = -1e+16
        LN_EPS = 1e-05

        def _gat_layer(h, mask, b):
            scores = jnp.einsum('...nd,...md->...nm', h, h)
            scores = jnp.where(mask, scores, NEG)
            attn = jax.nn.softmax(scores, axis=-1)
            return jnp.einsum('...nm,...md->...nd', attn, h) + b
        B, N, C = x.shape
        H, D, _ = Wh.shape
        mask = graph + jnp.eye(N, dtype=graph.dtype) > 0
        h = jnp.einsum('bnc,hdc->bhnd', x, Wh)
        out_h = _gat_layer(h, mask[None, None], bh[None, :, None, :])
        cat = jnp.transpose(out_h, (0, 2, 1, 3)).reshape(B, N, H * D)
        z = jax.nn.leaky_relu(cat, negative_slope=0.2)
        h2 = jnp.einsum('bnk,dk->bnd', z, Wo)
        out2 = _gat_layer(h2, mask[None], bo)
        z2 = jax.nn.leaky_relu(out2, negative_slope=0.2)
        mu = jnp.mean(z2, axis=-1, keepdims=True)
        var = jnp.mean(jnp.square(z2 - mu), axis=-1, keepdims=True)
        out = (z2 - mu) * jax.lax.rsqrt(var + LN_EPS) * gamma + beta
        return out

    x = _layernorm(x + _L0_gnn_ref(x, L0_gnn_W, L0_gnn_a, adj), axis=-1)
    x = _layernorm(x + _L1_gnn_ref(x, L1_gnn_w0, L1_gnn_b0, L1_gnn_wa, L1_gnn_ba, adj), axis=-1)
    x = _layernorm(x + _L2_gnn_ref(x, adj, L2_gnn_W, L2_gnn_a), axis=-1)
    x = _layernorm(x + _L3_gnn_ref(x, adj, L3_gnn_Wh, L3_gnn_bh, L3_gnn_Wo, L3_gnn_bo, L3_gnn_gamma, L3_gnn_beta), axis=-1)
    return x


_drawn_inputs = setup_inputs


def setup_inputs(seed=0):
    import zlib

    import numpy as np

    out = dict(_drawn_inputs(seed))
    spreads = {'L3_gnn_bh': (0.0, 0.1),
     'L3_gnn_bo': (0.0, 0.1),
     'L3_gnn_gamma': (1.0, 0.2),
     'L3_gnn_beta': (0.0, 0.1)}
    factors = {}
    for name, (base, spread) in spreads.items():
        noise = np.random.default_rng([zlib.crc32(name.encode()), seed]).standard_normal(out[name].shape)
        drawn = base * np.exp(spread * noise) if base else spread * noise
        out[name] = jnp.asarray(drawn.astype(out[name].dtype))
    for name, factor in factors.items():
        out[name] = (out[name] * factor).astype(out[name].dtype)
    return out
```

```python
from contextlib import ExitStack

import concourse.bass as bass
from concourse import mybir

F32 = mybir.dt.float32
F32R = mybir.dt.float32r
I32 = mybir.dt.int32
ALU = mybir.AluOpType
ACT = mybir.ActivationFunctionType
AX = mybir.AxisListType

BATCH, NODES, DIM = 16, 1024, 64
P = 128
TILES = NODES // P
HALF = 512
HALVES = NODES // HALF
PER_BANK = TILES // HALVES
HEADS = 4
AUG = DIM + 1
WIDE = 128
SLOPE = 0.2
EPS = 1e-5
INV_SQRT2 = 0.7071067811865476


def wait(engine, semaphore, count):
    if not isinstance(count, int) or count > 0:
        engine.wait_ge(semaphore, count)


def over_nodes(column):
    return column.unsqueeze(2).to_broadcast([P, TILES, DIM])


def over_tiles(row):
    return row.unsqueeze(1).to_broadcast([P, TILES, DIM])


class Memory:

    def __init__(self, nc, stack, stage):
        self.nc, self.stack, self.stage = nc, stack, stage
        self.semaphores = []
        stack.callback(self.release_semaphores)

    def sbuf(self, name, shape, dtype=F32):
        return self.stack.enter_context(self.nc.sbuf_tensor(f"{self.stage}_{name}", shape, dtype))

    def psum(self, name, shape=(P, NODES), dtype=F32):
        return self.stack.enter_context(self.nc.psum_tensor(f"{self.stage}_{name}", list(shape), dtype))

    def semaphore(self, name):
        self.semaphores.append(self.nc.alloc_semaphore(f"{self.stage}_{name}"))
        return self.semaphores[-1]

    def release_semaphores(self):
        if self.semaphores:
            self.nc.clear_and_free_semaphores(self.semaphores)
            self.nc.all_engine_barrier()


class LayerNorm:

    def __init__(self, mem, name, exponent):
        self.exponent = exponent
        self.y = mem.sbuf(f"{name}_y", [P, TILES, DIM])
        self.centred = mem.sbuf(f"{name}_centred", [P, TILES, DIM])
        self.squares = mem.sbuf(f"{name}_squares", [P, TILES, DIM])
        self.sums = mem.sbuf(f"{name}_sums", [P, TILES])
        self.minus_mean = mem.sbuf(f"{name}_minus_mean", [P, TILES])
        self.sum_squares = mem.sbuf(f"{name}_sum_squares", [P, TILES])
        self.variances = mem.sbuf(f"{name}_variances", [P, TILES])
        self.rstd = mem.sbuf(f"{name}_rstd", [P, TILES])
        self.y_ready = mem.semaphore(f"{name}_y_ready")
        self.sums_ready = mem.semaphore(f"{name}_sums_ready")
        self.mean_ready = mem.semaphore(f"{name}_mean_ready")
        self.centred_ready = mem.semaphore(f"{name}_centred_ready")
        self.squares_ready = mem.semaphore(f"{name}_squares_ready")
        self.sum_squares_ready = mem.semaphore(f"{name}_sum_squares_ready")
        self.variance_ready = mem.semaphore(f"{name}_variance_ready")
        self.rstd_ready = mem.semaphore(f"{name}_rstd_ready")

    def mean(self, dve, n):
        dve.wait_ge(self.y_ready, n)
        dve.tensor_reduce(self.sums[:, :], self.y[:, :, :], AX.X, ALU.add).then_inc(self.sums_ready, 1)
        dve.wait_ge(self.sums_ready, n)
        dve.tensor_scalar(self.minus_mean[:, :], self.sums[:, :], -1.0 / DIM, None, ALU.mult)\
           .then_inc(self.mean_ready, 1)

    def centre(self, pool, n):
        pool.wait_ge(self.mean_ready, n)
        pool.tensor_tensor(self.centred[:, :, :], self.y[:, :, :], over_nodes(self.minus_mean[:, :]), ALU.add)\
            .then_inc(self.centred_ready, 1)

    def square(self, act, n):
        act.wait_ge(self.centred_ready, n)
        act.activation(self.squares[:, :, :], self.centred[:, :, :], ACT.Square).then_inc(self.squares_ready, 1)

    def variance(self, dve, n):
        dve.wait_ge(self.squares_ready, n)
        dve.tensor_reduce(self.sum_squares[:, :], self.squares[:, :, :], AX.X, ALU.add)\
           .then_inc(self.sum_squares_ready, 1)
        dve.wait_ge(self.sum_squares_ready, n)
        dve.tensor_scalar(self.variances[:, :], self.sum_squares[:, :], 1.0 / DIM, EPS, ALU.mult, ALU.add)\
           .then_inc(self.variance_ready, 1)

    def inverse_deviation(self, pool, n):
        pool.wait_ge(self.variance_ready, n)
        pool.tensor_tensor(self.rstd[:, :], self.variances[:, :], self.exponent[:, :], ALU.pow)\
            .then_inc(self.rstd_ready, 1)




def setup(nc, ins, keep):
    with ExitStack() as stack:
        mem = Memory(nc, stack, "setup")
        adj = mem.sbuf("adj", [P, TILES, NODES], I32)
        rows = mem.sbuf("rows", [P, TILES, NODES])
        ones = mem.sbuf("ones", [P, P], F32R)
        degree = mem.psum("degree")
        turned = [mem.psum(f"turned{k}") for k in range(2)]
        loaded, consts, masked, turned_full, copied, degree_ready = (
            mem.semaphore(n) for n in ("loaded", "consts", "masked", "turned_full", "copied", "degree_ready"))
        x_loaded, empty_ready = mem.semaphore("x_loaded"), mem.semaphore("empty_ready")
        x_v = ins["x"].rearrange("b (t p) d -> p b t d", p=P)
        adj_v = ins["adj"].rearrange("(t p) j -> p t j", p=P)
        with nc.Block() as block:

            @block.sync
            def _(sp):
                for t in range(TILES):
                    sp.dma_start(adj[:, t, :], adj_v[:, t, :]).then_inc(loaded, 16)
                for b in range(BATCH):
                    sp.dma_start(keep.x[:, b, :, :], x_v[:, b, :, :]).then_inc(x_loaded, 16)
                sp.wait_ge(x_loaded, 16 * BATCH)

            @block.gpsimd
            def _(pool):
                pool.memset(keep.ident[:, :], 0.0).then_inc(consts, 1)
                pool.memset(keep.minus_half[:, :], -0.5).then_inc(consts, 1)
                pool.memset(ones[:, :].bitcast(F32), 1.0).then_inc(consts, 1)
                pool.memset(keep.ones[:, :], 1.0).then_inc(consts, 1)
                pool.memset(keep.x[:, BATCH, :, :], 0.0).then_inc(consts, 1)
                pool.wait_ge(consts, 5)
                pool.affine_select(out=keep.ident[:, :], in_=keep.ident[:, :], compare_op=ALU.not_equal, fill=1.0,
                                   base=0, pattern=[[-1, P]], channel_multiplier=1).then_inc(consts, 1)

            @block.vector
            def _(dve):
                dve.wait_ge(loaded, 16 * TILES)
                for t in range(TILES):
                    dve.tensor_scalar(rows[:, t, :], adj[:, t, :], 0.0, None, ALU.is_gt).then_inc(masked, 1)
                dve.wait_ge(degree_ready, 1)
                dve.tensor_scalar(keep.empty[:, :], degree[0:1, :], 0.0, None, ALU.is_equal).then_inc(empty_ready, 1)

            @block.tensor
            def _(pe):
                pe.wait_ge(consts, 6)
                pe.wait_ge(masked, TILES)
                for j in range(TILES):
                    if j >= 2:
                        pe.wait_ge(copied, j - 1)
                    for i in range(TILES):
                        last = pe.transpose(turned[j % 2][:, i * P:(i + 1) * P], rows[:, i, j * P:(j + 1) * P],
                                            keep.ident[:, :])
                    last.then_inc(turned_full, 1)
                for j in range(TILES):
                    pe.wait_ge(copied, j + 1)
                    for h in range(HALVES):
                        last = pe.matmul(degree[:, h * HALF:(h + 1) * HALF], ones[:, :],
                                         keep.mask[:, j, h * HALF:(h + 1) * HALF],
                                         start=(j == 0), stop=(j == TILES - 1))
                last.then_inc(degree_ready, 1)

            @block.scalar
            def _(act):
                for j in range(TILES):
                    act.wait_ge(turned_full, j + 1)
                    act.activation(keep.mask[:, j, :], turned[j % 2][:, :], ACT.Copy).then_inc(copied, 1)




def additive_layer(nc, stage, keep, w_in, a_in):
    with ExitStack() as stack:
        mem = Memory(nc, stack, stage)
        sb, sem = mem.sbuf, mem.semaphore
        RING = 4
        w = sb("w", [DIM, DIM])
        w_turned = sb("w_turned", [DIM, DIM])
        a_cols = sb("a_cols", [DIM, 2])
        a_wide = sb("a_wide", [DIM, 2 * P + 1])
        w_aug = sb("w_aug", [DIM, AUG])
        w_wide = sb("w_wide", [DIM, 2 * P])
        x_stage = sb("x_stage", [P, TILES + 1, DIM])
        x_turned = sb("x_turned", [DIM, NODES])
        hidden = sb("hidden", [P, TILES, AUG])
        minus_top = sb("minus_top", [P, 1])
        top = sb("top", [P, 1])
        below = sb("below", [P, TILES])
        low = sb("low", [P, TILES])
        gain = [sb(f"gain{k}", [P, TILES]) for k in range(2)]
        above = sb("above", [P, NODES])
        row = [sb(f"row{k}", [P, NODES]) for k in range(2)]
        values = [sb(f"values{k}", [P, TILES, WIDE]) for k in range(2)]
        totals = sb("totals", [1, AUG])
        weights = [sb(f"weights{k}", [P, NODES]) for k in range(RING)]
        recip = sb("recip", [P, TILES])
        mixed = sb("mixed", [P, TILES, DIM])
        negated = sb("negated", [P, TILES, DIM])
        expd = sb("expd", [P, TILES, DIM])
        elu = sb("elu", [P, TILES, DIM])
        norm = LayerNorm(mem, "norm", keep.minus_half)

        ps_x = mem.psum("ps_x")
        ps_s1 = mem.psum("ps_s1")
        ps_s2 = mem.psum("ps_s2")
        ps_out = mem.psum("ps_out")

        empty_tile = sem("empty_tile")
        loaded, w_full, w_ready, prod_full, prod_ready = (
            sem(n) for n in ("loaded", "w_full", "w_ready", "prod_full", "prod_ready"))
        staged, x_full, x_ready, s2_full, s1_full, hidden_full, hidden_ready = (
            sem(n) for n in ("staged", "x_full", "x_ready", "s2_full", "s1_full", "hidden_full", "hidden_ready"))
        minus_top_ready, top_ready, below_ready, gain_ready, low_ready, above_ready, row_ready = (
            sem(n) for n in ("minus_top_ready", "top_ready", "below_ready", "gain_ready", "low_ready",
                             "above_ready", "row_ready"))
        values_ready, totals_full, totals_ready = sem("values_ready"), sem("totals_full"), sem("totals_ready")
        weights_ready, weights_used, out_full = sem("weights_ready"), sem("weights_used"), sem("out_full")
        recip_ready, mixed_ready, negated_ready, expd_ready, elu_ready, x_written = (
            sem(n) for n in ("recip_ready", "mixed_ready", "negated_ready", "expd_ready", "elu_ready", "x_written"))

        def tile_cols(t):
            return slice(t * WIDE, t * WIDE + AUG)

        def by_tile(psum, a, b):
            return psum[:, :].rearrange("p (t c) -> p t c", c=WIDE)[:, :, a:b]

        with nc.Block() as block:

            @block.sync
            def _(sp):
                sp.dma_start(w[:, :], w_in).then_inc(loaded, 16)
                for k in range(2):
                    sp.dma_start(a_cols[:, k:k + 1], a_in[k * DIM:(k + 1) * DIM, :]).then_inc(loaded, 16)

            @block.gpsimd
            def _(pool):
                pool.memset(x_stage[:, TILES, :], 0.0).then_inc(empty_tile, 1)
                for s in range(2):
                    pool.memset(values[s][:, :, AUG:WIDE], 0.0).then_inc(empty_tile, 1)
                pool.memset(totals[:, DIM:AUG], float(NODES)).then_inc(totals_ready, 1)

                def stage_x(b):
                    wait(pool, x_full, b)
                    pool.tensor_copy(x_stage[:, 0:TILES, :], keep.x[:, b, :, :]).then_inc(staged, 1)

                def scale_values(b, s):
                    pool.wait_ge(low_ready, b + 1)
                    wait(pool, weights_used, TILES * (b - 1))
                    pool.tensor_tensor(values[s][:, :, 0:DIM], hidden[:, :, 0:DIM], over_nodes(low[:, :]),
                                       ALU.mult).then_inc(values_ready, 1)
                    pool.tensor_copy(values[s][:, :, DIM:AUG], low[:, :].unsqueeze(2)).then_inc(values_ready, 1)

                def residual(b):
                    pool.wait_ge(totals_ready, 1)
                    pool.wait_ge(elu_ready, b + 1)
                    pool.tensor_tensor(norm.y[:, :, :], elu[:, :, :], keep.x[:, b, :, :], ALU.add)\
                        .then_inc(norm.y_ready, 1)
                    norm.centre(pool, b + 1)

                def write_x(b):
                    norm.inverse_deviation(pool, b + 1)
                    pool.wait_ge(totals_ready, 1)
                    pool.wait_ge(norm.rstd_ready, b + 1)
                    pool.tensor_tensor(keep.x[:, b, :, :], norm.centred[:, :, :], over_nodes(norm.rstd[:, :]),
                                       ALU.mult).then_inc(x_written, 1)

                def step(b, s, first=False):
                    stage_x(b + 1)
                    if not first:
                        residual(b - 1)
                    if not first:
                        write_x(b - 1)
                    scale_values(b + 1, 1 - s)

                stage_x(0)
                scale_values(0, 0)
                step(0, 0, first=True)
                with pool.Fori(0, (BATCH - 2) // 2) as i:
                    step(2 * i + 1, 1)
                    step(2 * i + 2, 0)
                step(BATCH - 1, 1)
                residual(BATCH - 1)
                write_x(BATCH - 1)
                pool.wait_ge(x_written, BATCH)

            @block.vector
            def _(dve):
                dve.wait_ge(loaded, 48)
                dve.tensor_copy(a_wide[:, 0:1], a_cols[:, 1:2]).then_inc(w_ready, 1)
                dve.tensor_copy(a_wide[:, 1:1 + P], a_cols[:, 0:1].to_broadcast([DIM, P])).then_inc(w_ready, 1)
                dve.tensor_copy(a_wide[:, 1 + P:1 + 2 * P], a_cols[:, 1:2].to_broadcast([DIM, P]))\
                   .then_inc(w_ready, 1)
                dve.wait_ge(w_full, 1)
                dve.tensor_copy(w_turned[:, :], ps_x[0:DIM, 0:DIM]).then_inc(w_ready, 1)
                dve.tensor_copy(w_aug[:, 0:DIM], w[:, :]).then_inc(w_ready, 1)
                dve.wait_ge(prod_full, 1)
                dve.tensor_copy(w_aug[:, DIM:AUG], ps_s1[0:DIM, 0:1]).then_inc(prod_ready, 1)
                dve.tensor_copy(w_wide[:, :], ps_s1[0:DIM, 1:1 + 2 * P]).then_inc(prod_ready, 1)

                def find_top(b):
                    dve.wait_ge(s2_full, b + 1)
                    dve.tensor_reduce(minus_top[:, :], ps_s2[:, :], AX.X, ALU.max, negate=True)\
                       .then_inc(minus_top_ready, 1)
                    dve.wait_ge(minus_top_ready, b + 1)
                    dve.tensor_scalar(top[:, :], minus_top[:, :], -1.0, None, ALU.mult).then_inc(top_ready, 1)

                def weigh(b, s, t):
                    if t == 0:
                        dve.wait_ge(row_ready, b + 1)
                        dve.wait_ge(gain_ready, b + 1)
                    wait(dve, weights_used, TILES * b + t - RING + 1)
                    dve.scalar_tensor_tensor(out=weights[t % RING][:, :], in0=row[s][:, :],
                                             scalar=gain[s][:, t:t + 1], in1=keep.mask[:, t, :].bitcast(F32),
                                             op0=ALU.max, op1=ALU.mult).then_inc(weights_ready, 1)

                def divide(b):
                    dve.wait_ge(out_full, b + 1)
                    dve.reciprocal(recip[:, :].unsqueeze(2), by_tile(ps_out, DIM, AUG)).then_inc(recip_ready, 1)
                    dve.wait_ge(recip_ready, b + 1)
                    wait(dve, negated_ready, b)
                    dve.tensor_tensor(mixed[:, :, :], by_tile(ps_out, 0, DIM), over_nodes(recip[:, :]),
                                      ALU.mult)\
                       .then_inc(mixed_ready, 1)

                def apply_elu(b):
                    dve.wait_ge(expd_ready, b + 1)
                    dve.scalar_tensor_tensor(out=elu[:, :, :], in0=expd[:, :, :], scalar=-1.0, in1=mixed[:, :, :],
                                             op0=ALU.add, op1=ALU.max).then_inc(elu_ready, 1)

                def step(b, s, first=False):
                    weigh(b, s, 0)
                    if not first:
                        divide(b - 1)
                    weigh(b, s, 1)
                    if not first:
                        apply_elu(b - 1)
                    weigh(b, s, 2)
                    find_top(b + 1)
                    weigh(b, s, 3)
                    if not first:
                        norm.mean(dve, b)
                    weigh(b, s, 4)
                    weigh(b, s, 5)
                    weigh(b, s, 6)
                    if not first:
                        norm.variance(dve, b)
                    weigh(b, s, 7)

                find_top(0)
                step(0, 0, first=True)
                with dve.Fori(0, (BATCH - 2) // 2) as i:
                    step(2 * i + 1, 1)
                    step(2 * i + 2, 0)
                step(BATCH - 1, 1)
                divide(BATCH - 1)
                apply_elu(BATCH - 1)
                norm.mean(dve, BATCH)
                norm.variance(dve, BATCH)

            @block.scalar
            def _(act):

                def copy_x(b):
                    act.wait_ge(x_full, b + 1)
                    act.activation(x_turned[:, :], ps_x[0:DIM, :], ACT.Copy).then_inc(x_ready, 1)

                def copy_hidden(b):
                    act.wait_ge(hidden_full, b + 1)
                    wait(act, values_ready, 2 * b)
                    wait(act, totals_full, b)
                    act.activation(hidden[:, :, :], by_tile(ps_x, 0, AUG), ACT.Copy).then_inc(hidden_ready, 1)

                def factors(b, s):
                    act.wait_ge(minus_top_ready, b + 1)
                    act.wait_ge(hidden_ready, b + 1)
                    act.activation(below[:, :], hidden[:, :, DIM:AUG].rearrange("p t c -> p (t c)"), ACT.Identity,
                                   bias=minus_top[:, 0:1]).then_inc(below_ready, 1)
                    act.wait_ge(top_ready, b + 1)
                    act.wait_ge(s1_full, b + 1)
                    act.activation(above[:, :], ps_s1[:, :], ACT.Relu, bias=top[:, 0:1]).then_inc(above_ready, 1)
                    act.wait_ge(below_ready, b + 1)
                    wait(act, weights_ready, TILES * (b - 1))
                    act.activation(gain[s][:, :], below[:, :], ACT.Exp, scale=1.0 - SLOPE).then_inc(gain_ready, 1)
                    act.activation(low[:, :], below[:, :], ACT.Exp, scale=SLOPE).then_inc(low_ready, 1)
                    act.wait_ge(above_ready, b + 1)
                    act.activation(row[s][:, :], above[:, :], ACT.Exp, scale=SLOPE - 1.0).then_inc(row_ready, 1)

                def copy_totals(b):
                    act.wait_ge(totals_full, b + 1)
                    wait(act, out_full, b)
                    act.activation(totals[:, 0:DIM], ps_s2[0:1, 0:DIM], ACT.Copy).then_inc(totals_ready, 1)

                def exp_of_negative(b):
                    act.wait_ge(mixed_ready, b + 1)
                    act.activation(negated[:, :, :], mixed[:, :, :], ACT.Relu, scale=-1.0).then_inc(negated_ready, 1)
                    act.wait_ge(negated_ready, b + 1)
                    wait(act, elu_ready, b)
                    act.activation(expd[:, :, :], negated[:, :, :], ACT.Exp, scale=-1.0).then_inc(expd_ready, 1)

                def step(b, s, first=False):
                    copy_x(b + 1)
                    if not first:
                        exp_of_negative(b - 1)
                    copy_hidden(b + 1)
                    factors(b + 1, 1 - s)
                    if not first:
                        norm.square(act, b)
                    copy_totals(b + 1)

                copy_x(0)
                copy_hidden(0)
                factors(0, 0)
                copy_totals(0)
                step(0, 0, first=True)
                with act.Fori(0, (BATCH - 2) // 2) as i:
                    step(2 * i + 1, 1)
                    step(2 * i + 2, 0)
                step(BATCH - 1, 1)
                exp_of_negative(BATCH - 1)
                norm.square(act, BATCH)

            @block.tensor
            def _(pe):
                pe.wait_ge(loaded, 48)
                pe.transpose(ps_x[0:DIM, 0:DIM], w[:, :], keep.ident[0:DIM, 0:DIM]).then_inc(w_full, 1)
                pe.wait_ge(w_ready, 5)
                pe.matmul(ps_s1[0:DIM, 0:2 * P + 1], w_turned[:, :], a_wide[:, :], start=True, stop=True)\
                  .then_inc(prod_full, 1)
                pe.wait_ge(prod_ready, 2)
                pe.wait_ge(empty_tile, 3)

                def turn_x(b):
                    pe.wait_ge(staged, b + 1)
                    wait(pe, hidden_ready, b)
                    for t in range(TILES):
                        last = pe.transpose(ps_x[:, t * P:(t + 1) * P],
                                            x_stage[:, t:t + 2, :].rearrange("p t c -> p (t c)"), keep.ident[:, :])
                    last.then_inc(x_full, 1)

                def project(b):
                    pe.wait_ge(x_ready, b + 1)
                    wait(pe, totals_ready, b + 1 if not isinstance(b, int) or b > 0 else 0)
                    for h in range(HALVES):
                        last = pe.matmul(ps_s2[:, h * HALF:(h + 1) * HALF], w_wide[:, P:2 * P],
                                         x_turned[:, h * HALF:(h + 1) * HALF], start=True, stop=True)
                    last.then_inc(s2_full, 1)
                    wait(pe, above_ready, b)
                    for h in range(HALVES):
                        last = pe.matmul(ps_s1[:, h * HALF:(h + 1) * HALF], w_wide[:, 0:P],
                                         x_turned[:, h * HALF:(h + 1) * HALF], start=True, stop=True)
                    last.then_inc(s1_full, 1)
                    for t in range(TILES):
                        last = pe.matmul(ps_x[:, tile_cols(t)], x_turned[:, t * P:(t + 1) * P], w_aug[:, :],
                                         start=True, stop=True)
                    last.then_inc(hidden_full, 1)

                def sum_up(b):
                    pe.wait_ge(hidden_ready, b + 1)
                    pe.wait_ge(top_ready, b + 1)
                    for t in range(TILES):
                        last = pe.matmul(ps_s2[0:1, 0:DIM], keep.ones[:, 0:1], hidden[:, t, 0:DIM],
                                         start=(t == 0), stop=(t == TILES - 1))
                    last.then_inc(totals_full, 1)

                def multiply(b, s, t):
                    if t == 0:
                        pe.wait_ge(values_ready, 2 * (b + 1))
                        wait(pe, mixed_ready, b)
                    pe.wait_ge(weights_ready, TILES * b + t + 1)
                    for i in range(TILES):
                        last = pe.matmul(ps_out[:, i * WIDE:(i + 1) * WIDE], weights[t % RING][:, i * P:(i + 1) * P],
                                         values[s][:, t, :], start=(t == 0 and i % PER_BANK == 0), stop=False,
                                         skip_group_check=True)
                    last.then_inc(weights_used, 1)

                def add_totals(b):
                    pe.wait_ge(totals_ready, b + 2)
                    for i in range(TILES):
                        last = pe.matmul(ps_out[:, tile_cols(i)], keep.empty[:, i * P:(i + 1) * P], totals[:, :],
                                         start=False, stop=True, skip_group_check=True)
                    last.then_inc(out_full, 1)

                def step(b, s):
                    multiply(b, s, 0)
                    turn_x(b + 1)
                    multiply(b, s, 1)
                    project(b + 1)
                    for t in range(2, TILES):
                        multiply(b, s, t)
                    add_totals(b)
                    sum_up(b + 1)

                turn_x(0)
                project(0)
                sum_up(0)
                step(0, 0)
                with pe.Fori(0, (BATCH - 2) // 2) as i:
                    step(2 * i + 1, 1)
                    step(2 * i + 2, 0)
                step(BATCH - 1, 1)




def dot_layer(nc, stage, keep, ins):
    with ExitStack() as stack:
        mem = Memory(nc, stack, stage)
        sb, sem = mem.sbuf, mem.semaphore
        RING = 4
        LAG = 2
        UNITS = HEADS + 1
        CAT = HEADS * DIM
        SLOTS = 3

        wh_in = sb("wh_in", [P, 2, DIM])
        wo_in = sb("wo_in", [DIM, CAT])
        wh = sb("wh", [DIM, HEADS, DIM])
        wh_twice = sb("wh_twice", [DIM, HEADS, P])
        wo = sb("wo", [P, 2, DIM])
        wo_twice = sb("wo_twice", [P, 2, P])
        rows_in = sb("rows_in", [P, 3, DIM])
        bh = sb("bh", [P, HEADS, DIM])
        minus_high = sb("minus_high", [P, 1])
        minus_sum = sb("minus_sum", [DIM, P], F32R)

        x_stage = sb("x_stage", [P, TILES + 1, DIM])
        x_turned = sb("x_turned", [DIM, NODES])
        high_high = [sb(f"high_high{k}", [P, NODES], F32R) for k in range(SLOTS)]
        low_high = [sb(f"low_high{k}", [P, NODES], F32R) for k in range(SLOTS)]
        high_one = [sb(f"high_one{k}", [AUG, NODES], F32R) for k in range(SLOTS)]
        low_norm = [sb(f"low_norm{k}", [AUG, NODES], F32R) for k in range(SLOTS)]
        values = [sb(f"values{k}", [P, TILES, WIDE]) for k in range(SLOTS)]
        squares = sb("squares", [DIM, NODES], F32R)
        weights = [sb(f"weights{k}", [P, NODES]) for k in range(RING)]
        recip = sb("recip", [P, TILES])
        mixed = sb("mixed", [P, TILES, DIM])
        biased = sb("biased", [P, TILES, DIM])
        cat = sb("cat", [P, TILES, CAT])
        cat_turned = sb("cat_turned", [P, 2, NODES])
        inner = LayerNorm(mem, "inner", keep.minus_half)
        outer = LayerNorm(mem, "outer", keep.minus_half)
        normed = sb("normed", [P, TILES, DIM])
        gained = sb("gained", [P, TILES, DIM])
        shifted = sb("shifted", [P, TILES, DIM])

        ps_scores = [mem.psum(f"ps_scores{k}") for k in range(2)]
        ps_out = mem.psum("ps_out")
        ps_prep = mem.psum("ps_prep")

        loaded, set_up, turned_full, turned_ready = (
            sem(n) for n in ("loaded", "set_up", "turned_full", "turned_ready"))
        staged, x_full, x_ready, cat_ready, cat_full, cat_turned_ready = (
            sem(n) for n in ("staged", "x_full", "x_ready", "cat_ready", "cat_full", "cat_turned_ready"))
        hidden_full, norm_full, values_full = sem("hidden_full"), sem("norm_full"), sem("values_full")
        high_ready, low_ready, low_copied, high_copied, squares_ready, norm_ready, values_ready = (
            sem(n) for n in ("high_ready", "low_ready", "low_copied", "high_copied", "squares_ready", "norm_ready",
                             "values_ready"))
        scores_full, exp_ready, weights_ready, weights_used = (
            sem(n) for n in ("scores_full", "exp_ready", "weights_ready", "weights_used"))
        recip_ready, mixed_ready, biased_ready = (sem(n) for n in ("recip_ready", "mixed_ready", "biased_ready"))
        normed_ready, gained_ready, shifted_ready, x_written = (
            sem(n) for n in ("normed_ready", "gained_ready", "shifted_ready", "x_written"))

        SECOND = HEADS
        SLOT = (0, 1, 0, 1, 2)

        def order(first):
            return (0, 1, 2, 3) if first else (0, 1, SECOND, 2, 3)

        def first_unit(b):
            return 0 if isinstance(b, int) and b == 0 else UNITS * b - 1

        class Step:

            def __init__(self, b, first=False, last=False):
                self.b, self.first, self.last = b, first, last
                self.kinds, self.unit0 = order(first), first_unit(b)

            def before(self, k):
                return self.kinds[k - 1] if k else HEADS - 1

            def after(self, k):
                return self.kinds[k + 1] if k + 1 < len(self.kinds) else 0

            def closes(self, k):
                return k + 1 == len(self.kinds)

        def run_all(engine, run):
            run(Step(0, first=True))
            with engine.Fori(1, BATCH - 1) as b:
                run(Step(b))
            run(Step(BATCH - 1, last=True))

        def final_unit():
            return first_unit(BATCH)

        with nc.Block() as block:

            @block.sync
            def _(sp):
                for g in range(2):
                    sp.dma_start(wh_in[:, g, :], ins["L3_gnn_Wh"][2 * g:2 * g + 2, :, :]
                                 .rearrange("h d c -> (h d) c")).then_inc(loaded, 16)
                sp.dma_start(wo_in[:, :], ins["L3_gnn_Wo"]).then_inc(loaded, 16)
                for h in range(HEADS):
                    sp.dma_start(bh[:, h, :], ins["L3_gnn_bh"][h:h + 1, :].to_broadcast([P, DIM])).then_inc(loaded, 16)
                for k, name in enumerate(("L3_gnn_bo", "L3_gnn_gamma", "L3_gnn_beta")):
                    sp.dma_start(rows_in[:, k, :], ins[name].unsqueeze(0).to_broadcast([P, DIM])).then_inc(loaded, 16)

            @block.gpsimd
            def _(pool):
                pool.memset(x_stage[:, TILES, :], 0.0).then_inc(set_up, 1)
                pool.wait_ge(set_up, 1)
                pool.memset(minus_high[:, :], -1.0).then_inc(set_up, 1)
                pool.wait_ge(set_up, 2)
                pool.memset(minus_high[DIM:P, :], 0.0).then_inc(set_up, 1)
                pool.wait_ge(set_up, 3)
                pool.memset(minus_sum[:, :].bitcast(F32), 0.0).then_inc(set_up, 1)
                pool.wait_ge(set_up, 4)
                pool.memset(minus_sum[:, DIM:AUG].bitcast(F32), -1.0).then_inc(set_up, 1)
                for s in range(SLOTS):
                    pool.wait_ge(set_up, 5 + 3 * s)
                    pool.memset(high_one[s][DIM:AUG, :].bitcast(F32), 1.0).then_inc(set_up, 1)
                    pool.wait_ge(set_up, 6 + 3 * s)
                    pool.memset(values[s][:, :, DIM:AUG], 1.0).then_inc(set_up, 1)
                    pool.memset(values[s][:, :, AUG:WIDE], 0.0).then_inc(set_up, 1)
                pool.wait_ge(loaded, 16 * (3 + HEADS + 3))

                def stage_x(b):
                    wait(pool, x_ready, b)
                    pool.tensor_copy(x_stage[:, 0:TILES, :], keep.x[:, b, :, :]).then_inc(staged, 1)

                def square(u, s):
                    pool.wait_ge(high_ready, u + 1)
                    wait(pool, norm_ready, u)
                    pool.tensor_tensor(squares[:, :], high_high[s][0:DIM, :].bitcast(F32),
                                       high_high[s][0:DIM, :].bitcast(F32), ALU.mult).then_inc(squares_ready, 1)

                def add_bias(u, kind):
                    pool.wait_ge(mixed_ready, u + 1)
                    row = rows_in[:, 0, :] if kind == SECOND else bh[:, kind, :]
                    pool.tensor_tensor(biased[:, :, :], mixed[:, :, :], over_tiles(row), ALU.add)\
                        .then_inc(biased_ready, 1)

                def inner_affine(n):
                    inner.inverse_deviation(pool, n)
                    pool.wait_ge(inner.rstd_ready, n)
                    pool.tensor_tensor(normed[:, :, :], inner.centred[:, :, :], over_nodes(inner.rstd[:, :]), ALU.mult)\
                        .then_inc(normed_ready, 1)
                    pool.wait_ge(normed_ready, n)
                    pool.tensor_tensor(gained[:, :, :], normed[:, :, :], over_tiles(rows_in[:, 1, :]), ALU.mult)\
                        .then_inc(gained_ready, 1)
                    pool.wait_ge(gained_ready, n)
                    pool.tensor_tensor(shifted[:, :, :], gained[:, :, :], over_tiles(rows_in[:, 2, :]), ALU.add)\
                        .then_inc(shifted_ready, 1)
                    pool.wait_ge(set_up, 1)
                    pool.wait_ge(shifted_ready, n)
                    pool.tensor_tensor(outer.y[:, :, :], shifted[:, :, :], keep.x[:, n - 1, :, :], ALU.add)\
                        .then_inc(outer.y_ready, 1)
                    outer.centre(pool, n)

                def write_x(n):
                    outer.inverse_deviation(pool, n)
                    pool.wait_ge(set_up, 1)
                    pool.wait_ge(outer.rstd_ready, n)
                    pool.tensor_tensor(keep.x[:, n - 1, :, :], outer.centred[:, :, :], over_nodes(outer.rstd[:, :]),
                                       ALU.mult).then_inc(x_written, 1)

                def run(st):
                    for k, kind in enumerate(st.kinds):
                        u = st.unit0 + k
                        if k == 0 and not st.last:
                            stage_x(st.b + 1)
                        if not (st.first and k == 0):
                            add_bias(u - 1, st.before(k))
                        if not (st.last and st.closes(k)):
                            square(u + 1, SLOT[st.after(k)])
                        if not st.first and k == 3:
                            inner.centre(pool, st.b)
                        if not st.first and k == 4:
                            inner_affine(st.b)
                            write_x(st.b)

                stage_x(0)
                square(0, SLOT[0])
                run_all(pool, run)
                u = final_unit()
                add_bias(u - 1, HEADS - 1)
                square(u, SLOT[SECOND])
                add_bias(u, SECOND)
                inner.centre(pool, BATCH)
                inner_affine(BATCH)
                write_x(BATCH)
                pool.wait_ge(x_written, BATCH)

            @block.vector
            def _(dve):
                dve.wait_ge(turned_full, 1)
                for copy in range(2):
                    dve.tensor_copy(wh_twice[:, :, copy * DIM:(copy + 1) * DIM],
                                    ps_prep[0:DIM, 0:CAT].rearrange("c (h d) -> c h d", h=HEADS))\
                       .then_inc(turned_ready, 1)
                    dve.tensor_copy(wo_twice[:, :, copy * DIM:(copy + 1) * DIM],
                                    ps_prep[:, HALF:HALF + 2 * DIM].rearrange("k (c d) -> k c d", c=2))\
                       .then_inc(turned_ready, 1)
                for t in range(TILES):
                    dve.tensor_tensor(keep.mask[:, t, t * P:(t + 1) * P],
                                      keep.mask[:, t, t * P:(t + 1) * P].bitcast(F32), keep.ident[:, :], ALU.max)\
                       .then_inc(turned_ready, 1)
                dve.wait_ge(turned_ready, 4 + TILES)
                dve.wait_ge(set_up, 5 + 3 * SLOTS)

                def split_low(u, s):
                    dve.wait_ge(high_ready, u + 1)
                    dve.scalar_tensor_tensor(out=low_high[s][:, :], in0=high_high[s][:, :].bitcast(F32),
                                             scalar=minus_high[:, 0:1], in1=ps_prep[:, :], op0=ALU.mult, op1=ALU.add)\
                       .then_inc(low_ready, 1)

                def copy_low(u, s):
                    dve.wait_ge(low_ready, u + 1)
                    dve.tensor_copy(low_norm[s][0:DIM, :], low_high[s][0:DIM, :].bitcast(F32))\
                       .then_inc(low_copied, 1)

                def mask(u, t):
                    dve.wait_ge(exp_ready, TILES * u + t + 1)
                    buf = weights[t % RING]
                    dve.tensor_tensor(buf[:, :], buf[:, :], keep.mask[:, t, :].bitcast(F32), ALU.mult)\
                       .then_inc(weights_ready, 1)

                def divide(u):
                    out = ps_out[:, :].rearrange("p (t c) -> p t c", c=WIDE)
                    dve.wait_ge(weights_used, TILES * (u + 1))
                    dve.reciprocal(recip[:, :].unsqueeze(2), out[:, :, DIM:AUG]).then_inc(recip_ready, 1)
                    dve.wait_ge(recip_ready, u + 1)
                    wait(dve, biased_ready, u)
                    dve.tensor_tensor(mixed[:, :, :], out[:, :, 0:DIM], over_nodes(recip[:, :]), ALU.mult)\
                       .then_inc(mixed_ready, 1)

                def leaky(u, kind):
                    dve.wait_ge(biased_ready, u + 1)
                    to = inner.y[:, :, :] if kind == SECOND else cat[:, :, kind * DIM:(kind + 1) * DIM]
                    dve.scalar_tensor_tensor(out=to, in0=biased[:, :, :], scalar=SLOPE, in1=biased[:, :, :],
                                             op0=ALU.mult, op1=ALU.max)\
                       .then_inc(inner.y_ready if kind == SECOND else cat_ready, 1)

                def run(st):
                    for k, kind in enumerate(st.kinds):
                        u, s = st.unit0 + k, SLOT[st.after(k)]
                        for t in range(TILES):
                            mask(u, t)
                            if t == 0 and not (st.first and k == 0):
                                divide(u - 1)
                            if t == 2 and not (st.first and k == 0):
                                leaky(u - 1, st.before(k))
                            if t == (3 if st.closes(k) else 1) and not (st.last and st.closes(k)):
                                split_low(u + 1, s)
                            if t == (4 if st.closes(k) else 2) and not (st.last and st.closes(k)):
                                copy_low(u + 1, s)
                            if not st.first and (k, t) == (3, 4):
                                inner.mean(dve, st.b)
                            if not st.first and (k, t) == (3, 7):
                                inner.variance(dve, st.b)
                            if not st.first and (k, t) == (4, 6):
                                outer.mean(dve, st.b)
                            if not st.first and (k, t) == (4, 7):
                                outer.variance(dve, st.b)

                split_low(0, SLOT[0])
                copy_low(0, SLOT[0])
                run_all(dve, run)
                u = final_unit()
                divide(u - 1)
                leaky(u - 1, HEADS - 1)
                split_low(u, SLOT[SECOND])
                copy_low(u, SLOT[SECOND])
                for t in range(TILES):
                    mask(u, t)
                divide(u)
                leaky(u, SECOND)
                inner.mean(dve, BATCH)
                inner.variance(dve, BATCH)
                outer.mean(dve, BATCH)
                outer.variance(dve, BATCH)

            @block.scalar
            def _(act):
                act.wait_ge(turned_ready, 4)
                act.activation(wh[:, :, :], wh_twice[:, :, 0:DIM], ACT.Copy).then_inc(turned_ready, 1)
                act.activation(wo[:, :, :], wo_twice[:, :, 0:DIM], ACT.Copy).then_inc(turned_ready, 1)

                def copy_x(b):
                    act.wait_ge(x_full, b + 1)
                    act.activation(x_turned[:, :], ps_prep[0:DIM, :], ACT.Copy).then_inc(x_ready, 1)

                def round_high(u, s):
                    act.wait_ge(hidden_full, u + 1)
                    act.activation(high_high[s][:, :], ps_prep[:, :], ACT.Copy).then_inc(high_ready, 1)

                def copy_high(u, s):
                    act.wait_ge(high_ready, u + 1)
                    act.activation(high_one[s][0:DIM, :], high_high[s][0:DIM, :].bitcast(F32), ACT.Copy)\
                       .then_inc(high_copied, 1)

                def copy_norm(u, s):
                    act.wait_ge(norm_full, u + 1)
                    act.activation(low_norm[s][DIM:AUG, :], ps_prep[DIM:AUG, :], ACT.Copy).then_inc(norm_ready, 1)

                def copy_values(u, s):
                    act.wait_ge(values_full, u + 1)
                    act.activation(values[s][:, :, 0:DIM], ps_prep[:, 0:HALF].rearrange("p (t d) -> p t d", d=DIM),
                                   ACT.Copy).then_inc(values_ready, 1)

                def copy_cat(b, c):
                    act.wait_ge(cat_full, 2 * b + c + 1)
                    act.activation(cat_turned[:, c, :], ps_prep[:, :], ACT.Copy).then_inc(cat_turned_ready, 1)

                def exp(u, t):
                    act.wait_ge(scores_full, TILES * u + t + 1)
                    wait(act, weights_used, TILES * u + t + 1 - RING)
                    act.activation(weights[t % RING][:, :], ps_scores[t % 2][:, :], ACT.Exp).then_inc(exp_ready, 1)

                def run(st):
                    for k, kind in enumerate(st.kinds):
                        u, s = st.unit0 + k, SLOT[st.after(k)]
                        at = (3, 4, 6, 7) if st.closes(k) else (1, 2, 4, 5)
                        for t in range(TILES):
                            exp(u, t)
                            if st.closes(k) and not st.last and t == 1:
                                copy_x(st.b + 1)
                            if not (st.last and st.closes(k)):
                                if t == at[0]:
                                    round_high(u + 1, s)
                                if t == at[1]:
                                    copy_high(u + 1, s)
                                if t == at[2]:
                                    copy_norm(u + 1, s)
                                if t == at[3]:
                                    copy_values(u + 1, s)
                            if not st.first and k == 0 and t >= 6:
                                copy_cat(st.b - 1, t - 6)
                            if not st.first and (k, t) == (3, 6):
                                inner.square(act, st.b)
                            if not st.first and (k, t) == (4, 7):
                                outer.square(act, st.b)

                copy_x(0)
                round_high(0, SLOT[0])
                copy_high(0, SLOT[0])
                copy_norm(0, SLOT[0])
                copy_values(0, SLOT[0])
                run_all(act, run)
                u, s = final_unit(), SLOT[SECOND]
                copy_cat(BATCH - 1, 0)
                copy_cat(BATCH - 1, 1)
                round_high(u, s)
                copy_high(u, s)
                copy_norm(u, s)
                copy_values(u, s)
                for t in range(TILES):
                    exp(u, t)
                inner.square(act, BATCH)
                outer.square(act, BATCH)

            @block.tensor
            def _(pe):
                pe.wait_ge(loaded, 16 * (3 + HEADS + 3))
                for g in range(2):
                    pe.transpose(ps_prep[0:DIM, g * P:(g + 1) * P], wh_in[:, g, :], keep.ident[:, :])
                for c in range(2):
                    last = pe.transpose(ps_prep[:, HALF + c * DIM:HALF + (c + 1) * DIM], wo_in[:, c * P:(c + 1) * P],
                                        keep.ident[0:DIM, 0:DIM])
                last.then_inc(turned_full, 1)
                pe.wait_ge(turned_ready, 6 + TILES)
                pe.wait_ge(set_up, 5 + 3 * SLOTS)

                def turn_x(b):
                    pe.wait_ge(staged, b + 1)
                    wait(pe, values_ready, first_unit(b) if not isinstance(b, int) or b > 0 else 0)
                    for t in range(TILES):
                        last = pe.transpose(ps_prep[:, t * P:(t + 1) * P],
                                            x_stage[:, t:t + 2, :].rearrange("p t c -> p (t c)"), keep.ident[:, :])
                    last.then_inc(x_full, 1)

                def turn_cat(b, c, made):
                    pe.wait_ge(cat_ready, HEADS * b + 2 * (c + 1))
                    if c == 0:
                        pe.wait_ge(values_ready, made)
                    else:
                        pe.wait_ge(cat_turned_ready, 2 * b + 1)
                    for t in range(TILES):
                        last = pe.transpose(ps_prep[:, t * P:(t + 1) * P], cat[:, t, c * P:(c + 1) * P],
                                            keep.ident[:, :])
                    last.then_inc(cat_full, 1)

                def hidden(u, kind, b):
                    if kind == SECOND:
                        pe.wait_ge(cat_turned_ready, 2 * (b + 1))
                    else:
                        pe.wait_ge(x_ready, b + 1)
                        wait(pe, values_ready, u)
                    for h in range(HALVES):
                        cols = slice(h * HALF, (h + 1) * HALF)
                        if kind == SECOND:
                            for c in range(2):
                                last = pe.matmul(ps_prep[:, cols], wo_twice[:, c, :], cat_turned[:, c, cols],
                                                 start=(c == 0), stop=(c == 1))
                        else:
                            last = pe.matmul(ps_prep[:, cols], wh_twice[:, kind, :], x_turned[:, cols],
                                             start=True, stop=True)
                    last.then_inc(hidden_full, 1)

                def norms(u):
                    pe.wait_ge(squares_ready, u + 1)
                    pe.wait_ge(low_ready, u + 1)
                    for h in range(HALVES):
                        cols = slice(h * HALF, (h + 1) * HALF)
                        last = pe.matmul(ps_prep[:, cols], minus_sum[:, :], squares[:, cols], start=True, stop=True)
                    last.then_inc(norm_full, 1)

                def value_rows(u, kind):
                    pe.wait_ge(norm_ready, u + 1)
                    for t in range(TILES):
                        out, nodes = ps_prep[:, t * DIM:(t + 1) * DIM], slice(t * P, (t + 1) * P)
                        if kind == SECOND:
                            for c in range(2):
                                last = pe.matmul(out, cat_turned[:, c, nodes], wo[:, c, :], start=(c == 0),
                                                 stop=(c == 1))
                        else:
                            last = pe.matmul(out, x_turned[:, nodes], wh[:, kind, :], start=True, stop=True)
                    last.then_inc(values_full, 1)

                def scores(u, s, t):
                    if t == 0:
                        pe.wait_ge(low_copied, u + 1)
                        pe.wait_ge(high_copied, u + 1)
                        pe.wait_ge(norm_ready, u + 1)
                    wait(pe, exp_ready, TILES * u + t - 1)
                    nodes = slice(t * P, (t + 1) * P)
                    for h in range(HALVES):
                        cols = slice(h * HALF, (h + 1) * HALF)
                        pe.matmul(ps_scores[t % 2][:, cols], low_high[s][:, nodes], high_high[s][:, cols],
                                  start=True, stop=False)
                        last = pe.matmul(ps_scores[t % 2][:, cols], high_one[s][:, nodes], low_norm[s][:, cols],
                                         start=False, stop=True)
                    last.then_inc(scores_full, 1)

                def multiply(u, s, t):
                    if t == 0:
                        pe.wait_ge(values_ready, u + 1)
                        wait(pe, mixed_ready, u)
                    pe.wait_ge(weights_ready, TILES * u + t + 1)
                    for i in range(TILES):
                        last = pe.matmul(ps_out[:, i * WIDE:(i + 1) * WIDE], weights[t % RING][:, i * P:(i + 1) * P],
                                         values[s][:, t, :], start=(t == 0 and i % PER_BANK == 0),
                                         stop=(t == TILES - 1), skip_group_check=True)
                    last.then_inc(weights_used, 1)

                def run(st):
                    for k, kind in enumerate(st.kinds):
                        u, after = st.unit0 + k, st.after(k)
                        batch = st.b + 1 if st.closes(k) else st.b - 1 if after == SECOND else st.b
                        at = (2, 5, 6) if st.closes(k) else (0, 3, 4)
                        for t in range(TILES):
                            scores(u, SLOT[kind], t)
                            if st.closes(k) and not st.last and t == 0:
                                turn_x(st.b + 1)
                            if not (st.last and st.closes(k)):
                                if t == at[0]:
                                    hidden(u + 1, after, batch)
                                if t == at[1]:
                                    norms(u + 1)
                                if t == at[2]:
                                    value_rows(u + 1, after)
                            if not st.first and k == 0 and t >= 5 and t < 7:
                                turn_cat(st.b - 1, t - 5, u + 2)
                            if t >= LAG:
                                multiply(u, SLOT[kind], t - LAG)
                            elif not (st.first and k == 0):
                                multiply(u - 1, SLOT[st.before(k)], TILES + t - LAG)

                turn_x(0)
                hidden(0, 0, 0)
                norms(0)
                value_rows(0, 0)
                run_all(pe, run)
                u, s = final_unit(), SLOT[SECOND]
                for t in range(TILES - LAG, TILES):
                    multiply(u - 1, SLOT[HEADS - 1], t)
                turn_cat(BATCH - 1, 0, u)
                turn_cat(BATCH - 1, 1, u)
                hidden(u, SECOND, BATCH - 1)
                norms(u)
                value_rows(u, SECOND)
                for t in range(TILES + LAG):
                    if t < TILES:
                        scores(u, s, t)
                    if t >= LAG:
                        multiply(u, s, t - LAG)




def feature_layer(nc, stage, keep, ins):
    with ExitStack() as stack:
        mem = Memory(nc, stack, stage)
        sb, sem = mem.sbuf, mem.semaphore
        BOTH = 2 * DIM
        scalars = sb("scalars", [P, 3])
        rows_in = sb("rows_in", [P, 2, DIM])
        scaled = sb("scaled", [P, TILES, DIM])
        positive = sb("positive", [P, TILES, DIM])
        decayed = sb("decayed", [P, TILES, DIM])
        soft = sb("soft", [P, TILES, DIM])
        feat = [sb(f"feat{k}", [P, TILES, DIM]) for k in range(2)]
        product = sb("product", [P, TILES, DIM])
        score = sb("score", [P, TILES, DIM])
        tile_top = sb("tile_top", [P, DIM])
        top = sb("top", [DIM, 1])
        top_diag = sb("top_diag", [DIM, DIM])
        shifted = sb("shifted", [P, TILES, DIM])
        exact = sb("exact", [P, TILES, BOTH])
        high = [sb(f"high{k}", [P, TILES, BOTH], F32R) for k in range(2)]
        rest = [sb(f"rest{k}", [P, TILES, BOTH], F32R) for k in range(2)]
        totals = sb("totals", [1, BOTH])
        recip = sb("recip", [P, TILES, DIM])
        mixed = sb("mixed", [P, TILES, DIM])
        norm = LayerNorm(mem, "norm", keep.minus_half)

        ps_top = mem.psum("ps_top", (P, HALF))
        ps_wide = mem.psum("ps_wide", (P, HALF))
        ps_total = mem.psum("ps_total", (P, HALF))
        ps_out = [mem.psum(f"ps_out{k}") for k in range(2)]

        loaded, scale_ready = sem("loaded"), sem("scale_ready")
        scaled_ready, positive_ready, decayed_ready, soft_ready = (
            sem(n) for n in ("scaled_ready", "positive_ready", "decayed_ready", "soft_ready"))
        feat_ready, product_ready, score_ready, tile_top_ready, top_full, top_ready, diag_ready, wide_full = (
            sem(n) for n in ("feat_ready", "product_ready", "score_ready", "tile_top_ready", "top_full", "top_ready",
                             "diag_ready", "wide_full"))
        shifted_ready, exp_ready, exact_ready, high_ready, rest_ready = (
            sem(n) for n in ("shifted_ready", "exp_ready", "exact_ready", "high_ready", "rest_ready"))
        total_full, totals_ready, out_full, recip_ready, mixed_ready, x_written = (
            sem(n) for n in ("total_full", "totals_ready", "out_full", "recip_ready", "mixed_ready", "x_written"))

        def out_half(s, h, a, b):
            return ps_out[s][:, h * HALF:(h + 1) * HALF].rearrange("p (t c) -> p t c", c=BOTH)[:, :, a:b]

        with nc.Block() as block:

            @block.sync
            def _(sp):
                sp.dma_start(scalars[:, 0:1], ins["L1_gnn_w0"].to_broadcast([P, 1])).then_inc(loaded, 16)
                sp.dma_start(scalars[:, 1:2], ins["L1_gnn_b0"].unsqueeze(0).to_broadcast([P, 1]))\
                  .then_inc(loaded, 16)
                sp.dma_start(rows_in[:, 0, :], ins["L1_gnn_wa"].unsqueeze(0).to_broadcast([P, DIM]))\
                  .then_inc(loaded, 16)
                sp.dma_start(rows_in[:, 1, :], ins["L1_gnn_ba"].unsqueeze(0).to_broadcast([P, DIM]))\
                  .then_inc(loaded, 16)

            @block.gpsimd
            def _(pool):
                pool.memset(totals[:, DIM:BOTH], float(NODES)).then_inc(totals_ready, 1)
                pool.wait_ge(loaded, 64)

                def score_nodes(b, s):
                    pool.wait_ge(soft_ready, b + 1)
                    wait(pool, total_full, b - 1)
                    pool.tensor_tensor(feat[s][:, :, :], positive[:, :, :], soft[:, :, :], ALU.add)\
                        .then_inc(feat_ready, 1)
                    pool.wait_ge(feat_ready, b + 1)
                    pool.tensor_tensor(product[:, :, :], feat[s][:, :, :], over_tiles(rows_in[:, 0, :]), ALU.mult)\
                        .then_inc(product_ready, 1)
                    wait(pool, shifted_ready, b)
                    pool.wait_ge(product_ready, b + 1)
                    pool.tensor_tensor(score[:, :, :], product[:, :, :], over_tiles(rows_in[:, 1, :]), ALU.add)\
                        .then_inc(score_ready, 1)

                def weigh_feat(b, s):
                    pool.wait_ge(exp_ready, b + 1)
                    wait(pool, rest_ready, b)
                    pool.tensor_tensor(exact[:, :, 0:DIM], exact[:, :, DIM:BOTH], feat[s][:, :, :], ALU.mult)\
                        .then_inc(exact_ready, 1)

                def residual(b):
                    pool.wait_ge(totals_ready, 1)
                    pool.wait_ge(mixed_ready, 2 * (b + 1))
                    pool.tensor_tensor(norm.y[:, :, :], mixed[:, :, :], keep.x[:, b, :, :], ALU.add)\
                        .then_inc(norm.y_ready, 1)
                    norm.centre(pool, b + 1)

                def write_x(b):
                    norm.inverse_deviation(pool, b + 1)
                    pool.wait_ge(totals_ready, 1)
                    pool.wait_ge(norm.rstd_ready, b + 1)
                    pool.tensor_tensor(keep.x[:, b, :, :], norm.centred[:, :, :], over_nodes(norm.rstd[:, :]),
                                       ALU.mult).then_inc(x_written, 1)

                def step(b, s, first=False):
                    score_nodes(b + 1, 1 - s)
                    if not first:
                        residual(b - 1)
                    weigh_feat(b + 1, 1 - s)
                    if not first:
                        write_x(b - 1)

                score_nodes(0, 0)
                weigh_feat(0, 0)
                step(0, 0, first=True)
                with pool.Fori(0, (BATCH - 2) // 2) as i:
                    step(2 * i + 1, 1)
                    step(2 * i + 2, 0)
                step(BATCH - 1, 1)
                residual(BATCH - 1)
                write_x(BATCH - 1)
                pool.wait_ge(x_written, BATCH)

            @block.vector
            def _(dve):
                dve.wait_ge(loaded, 64)
                dve.tensor_scalar(scalars[:, 2:3], scalars[:, 0:1], INV_SQRT2, None, ALU.mult)\
                   .then_inc(scale_ready, 1)

                def find_tile_top(b):
                    dve.wait_ge(score_ready, b + 1)
                    dve.tensor_reduce(tile_top[:, :], score[:, :, :].rearrange("p t d -> p d t"), AX.X, ALU.max)\
                       .then_inc(tile_top_ready, 1)

                def find_top(b):
                    dve.wait_ge(top_full, b + 1)
                    dve.tensor_reduce(top[:, :], ps_top[0:DIM, 0:P], AX.X, ALU.max).then_inc(top_ready, 1)
                    dve.wait_ge(top_ready, b + 1)
                    dve.tensor_scalar(top_diag[:, :], keep.ident[0:DIM, 0:DIM], top[:, 0:1], None, ALU.mult)\
                       .then_inc(diag_ready, 1)

                def shift(b):
                    dve.wait_ge(wide_full, b + 1)
                    wait(dve, exp_ready, b)
                    dve.tensor_tensor(shifted[:, :, :], score[:, :, :], over_tiles(ps_wide[:, 0:DIM]), ALU.subtract)\
                       .then_inc(shifted_ready, 1)

                def split(b, s):
                    dve.wait_ge(exact_ready, b + 1)
                    wait(dve, out_full, HALVES * (b - 1))
                    dve.tensor_copy(high[s][:, :, :], exact[:, :, :]).then_inc(high_ready, 1)
                    dve.wait_ge(high_ready, b + 1)
                    dve.tensor_tensor(rest[s][:, :, :], exact[:, :, :], high[s][:, :, :].bitcast(F32), ALU.subtract)\
                       .then_inc(rest_ready, 1)

                def divide(b, s, h):
                    dve.wait_ge(out_full, HALVES * b + h + 1)
                    nodes = slice(h * PER_BANK, (h + 1) * PER_BANK)
                    dve.reciprocal(recip[:, nodes, :], out_half(s, h, DIM, BOTH)).then_inc(recip_ready, 1)
                    dve.wait_ge(recip_ready, HALVES * b + h + 1)
                    wait(dve, norm.y_ready, b)
                    dve.tensor_tensor(mixed[:, nodes, :], out_half(s, h, 0, DIM), recip[:, nodes, :], ALU.mult)\
                       .then_inc(mixed_ready, 1)

                def step(b, s, first=False):
                    find_tile_top(b + 1)
                    if not first:
                        divide(b - 1, 1 - s, 1)
                    find_top(b + 1)
                    if not first:
                        norm.mean(dve, b)
                    shift(b + 1)
                    if not first:
                        norm.variance(dve, b)
                    split(b + 1, 1 - s)
                    divide(b, s, 0)

                find_tile_top(0)
                find_top(0)
                shift(0)
                split(0, 0)
                step(0, 0, first=True)
                with dve.Fori(0, (BATCH - 2) // 2) as i:
                    step(2 * i + 1, 1)
                    step(2 * i + 2, 0)
                step(BATCH - 1, 1)
                divide(BATCH - 1, 1, 1)
                norm.mean(dve, BATCH)
                norm.variance(dve, BATCH)

            @block.scalar
            def _(act):
                act.wait_ge(scale_ready, 1)

                def softplus(b):
                    act.activation(scaled[:, :, :], keep.x[:, b, :, :], ACT.Abs, bias=scalars[:, 1:2],
                                   scale=scalars[:, 2:3]).then_inc(scaled_ready, 1)
                    act.wait_ge(scale_ready, 1)
                    wait(act, feat_ready, b)
                    act.activation(positive[:, :, :], keep.x[:, b, :, :], ACT.Relu, bias=scalars[:, 1:2],
                                   scale=scalars[:, 2:3]).then_inc(positive_ready, 1)
                    act.wait_ge(scaled_ready, b + 1)
                    act.activation(decayed[:, :, :], scaled[:, :, :], ACT.Exp, scale=-1.0).then_inc(decayed_ready, 1)
                    act.wait_ge(decayed_ready, b + 1)
                    act.activation(soft[:, :, :], decayed[:, :, :], ACT.Ln, bias=1.0).then_inc(soft_ready, 1)

                def exp(b):
                    act.wait_ge(shifted_ready, b + 1)
                    wait(act, rest_ready, b)
                    act.activation(exact[:, :, DIM:BOTH], shifted[:, :, :], ACT.Exp).then_inc(exp_ready, 1)

                def copy_totals(b):
                    act.wait_ge(total_full, b + 1)
                    wait(act, out_full, HALVES * b)
                    act.activation(totals[:, 0:DIM], ps_total[0:1, 0:DIM], ACT.Copy).then_inc(totals_ready, 1)

                def step(b, first=False):
                    softplus(b + 1)
                    exp(b + 1)
                    if not first:
                        norm.square(act, b)
                    copy_totals(b + 1)

                softplus(0)
                exp(0)
                copy_totals(0)
                step(0, first=True)
                with act.Fori(1, BATCH) as b:
                    step(b)
                norm.square(act, BATCH)

            @block.tensor
            def _(pe):

                def turn_top(b):
                    pe.wait_ge(tile_top_ready, b + 1)
                    wait(pe, top_ready, b)
                    pe.matmul(ps_top[0:DIM, 0:P], tile_top[:, :], keep.ident[:, :], start=True, stop=True)\
                      .then_inc(top_full, 1)

                def spread_top(b):
                    pe.wait_ge(diag_ready, b + 1)
                    wait(pe, shifted_ready, b)
                    pe.matmul(ps_wide[:, 0:DIM], keep.ones[0:DIM, :], top_diag[:, :], start=True, stop=True)\
                      .then_inc(wide_full, 1)

                def sum_up(b, s):
                    pe.wait_ge(feat_ready, b + 1)
                    wait(pe, totals_ready, b + 1)
                    for t in range(TILES):
                        last = pe.matmul(ps_total[0:1, 0:DIM], keep.ones[:, 0:1], feat[s][:, t, :],
                                         start=(t == 0), stop=(t == TILES - 1))
                    last.then_inc(total_full, 1)

                def multiply(b, s, h):
                    if h == 0:
                        pe.wait_ge(rest_ready, b + 1)
                        pe.wait_ge(totals_ready, b + 2)
                    wait(pe, mixed_ready, HALVES * (b - 1) + h + 1)
                    for i in range(h * PER_BANK, (h + 1) * PER_BANK):
                        out = ps_out[s][:, i * BOTH:(i + 1) * BOTH]
                        for t in range(TILES):
                            for part in (high[s], rest[s]):
                                pe.matmul(out, keep.mask[:, t, i * P:(i + 1) * P], part[:, t, :],
                                          start=(t == 0 and part is high[s]), stop=False)
                        last = pe.matmul(out, keep.empty[:, i * P:(i + 1) * P], totals[:, :], start=False, stop=True)
                    last.then_inc(out_full, 1)

                def step(b, s):
                    multiply(b, s, 0)
                    turn_top(b + 1)
                    spread_top(b + 1)
                    multiply(b, s, 1)
                    sum_up(b + 1, 1 - s)

                turn_top(0)
                spread_top(0)
                sum_up(0, 0)
                step(0, 0)
                with pe.Fori(0, (BATCH - 2) // 2) as i:
                    step(2 * i + 1, 1)
                    step(2 * i + 2, 0)
                step(BATCH - 1, 1)




def store(nc, keep, out):
    with ExitStack() as stack:
        mem = Memory(nc, stack, "store")
        stored = mem.semaphore("stored")
        out_v = out.rearrange("b (t p) d -> p b t d", p=P)
        with nc.Block() as block:

            @block.sync
            def _(sp):
                sp.dma_start(out_v, keep.x[:, 0:BATCH, :, :]).then_inc(stored, 16)
                sp.wait_ge(stored, 16)


class Keep:

    def __init__(self, mem):
        self.x = mem.sbuf("x", [P, BATCH + 1, TILES, DIM])
        self.mask = mem.sbuf("mask", [P, TILES, NODES], F32R)
        self.empty = mem.sbuf("empty", [1, NODES])
        self.ident = mem.sbuf("ident", [P, P])
        self.ones = mem.sbuf("ones", [P, P])
        self.minus_half = mem.sbuf("minus_half", [P, TILES])


def build(nc, ins, out):
    with ExitStack() as stack:
        keep = Keep(Memory(nc, stack, "keep"))
        setup(nc, ins, keep)
        additive_layer(nc, "first", keep, ins["L0_gnn_W"], ins["L0_gnn_a"])
        feature_layer(nc, "second", keep, ins)
        additive_layer(nc, "third", keep, ins["L2_gnn_W"], ins["L2_gnn_a"])
        dot_layer(nc, "fourth", keep, ins)
        store(nc, keep, out)


INPUTS = ["x", "adj", "L0_gnn_W", "L0_gnn_a", "L1_gnn_w0", "L1_gnn_b0", "L1_gnn_wa", "L1_gnn_ba", "L2_gnn_W",
          "L2_gnn_a", "L3_gnn_Wh", "L3_gnn_bh", "L3_gnn_Wo", "L3_gnn_bo", "L3_gnn_gamma", "L3_gnn_beta"]


def kernel(**inputs):
    import numpy as np
    import concourse.bacc as bacc
    from concourse.bass_utils import run_bass_kernel_spmd

    nc = bacc.Bacc("TRN2", target_bir_lowering=False, num_devices=1)
    arrays, ins = {}, {}
    for name in INPUTS:
        a = np.ascontiguousarray(inputs[name])
        arrays[f"in_{name}"] = a
        ins[name] = nc.dram_tensor(f"in_{name}", a.shape, mybir.dt.from_np(a.dtype), kind="ExternalInput").ap()
    out = nc.dram_tensor("out", (BATCH, NODES, DIM), F32, kind="ExternalOutput").ap()
    build(nc, ins, out)
    result = run_bass_kernel_spmd(nc, [arrays], core_ids=[0])
    return result.results[0]["out"]
```

```python
from contextlib import ExitStack

import concourse.bass as bass
from concourse import mybir

F32 = mybir.dt.float32
F32R = mybir.dt.float32r
I32 = mybir.dt.int32
ALU = mybir.AluOpType
ACT = mybir.ActivationFunctionType
AX = mybir.AxisListType

BATCH, NODES, DIM = 16, 1024, 64
P = 128
TILES = NODES // P
HALF = 512
HALVES = NODES // HALF
PER_BANK = TILES // HALVES
HEADS = 4
AUG = DIM + 1
WIDE = 128
SLOPE = 0.2
EPS = 1e-5
INV_SQRT2 = 0.7071067811865476


def wait(engine, semaphore, count):
    if not isinstance(count, int) or count > 0:
        engine.wait_ge(semaphore, count)


def over_nodes(column):
    return column.unsqueeze(2).to_broadcast([P, TILES, DIM])


def over_tiles(row):
    return row.unsqueeze(1).to_broadcast([P, TILES, DIM])


def x_rows(ins):
    return ins["x"].rearrange("b (t p) d -> p b t d", p=P)


class Memory:

    def __init__(self, nc, stack, stage):
        self.nc, self.stack, self.stage = nc, stack, stage
        self.semaphores = []
        stack.callback(self.release_semaphores)

    def sbuf(self, name, shape, dtype=F32):
        return self.stack.enter_context(self.nc.sbuf_tensor(f"{self.stage}_{name}", shape, dtype))

    def psum(self, name, shape=(P, NODES), dtype=F32):
        return self.stack.enter_context(self.nc.psum_tensor(f"{self.stage}_{name}", list(shape), dtype))

    def semaphore(self, name):
        self.semaphores.append(self.nc.alloc_semaphore(f"{self.stage}_{name}"))
        return self.semaphores[-1]

    def release_semaphores(self):
        if self.semaphores:
            self.nc.clear_and_free_semaphores(self.semaphores)
            self.nc.all_engine_barrier()


class LayerNorm:

    def __init__(self, mem, name, exponent):
        self.exponent = exponent
        self.y = mem.sbuf(f"{name}_y", [P, TILES, DIM])
        self.centred = mem.sbuf(f"{name}_centred", [P, TILES, DIM])
        self.squares = mem.sbuf(f"{name}_squares", [P, TILES, DIM])
        self.sums = mem.sbuf(f"{name}_sums", [P, TILES])
        self.minus_mean = mem.sbuf(f"{name}_minus_mean", [P, TILES])
        self.sum_squares = mem.sbuf(f"{name}_sum_squares", [P, TILES])
        self.variances = mem.sbuf(f"{name}_variances", [P, TILES])
        self.rstd = mem.sbuf(f"{name}_rstd", [P, TILES])
        self.y_ready = mem.semaphore(f"{name}_y_ready")
        self.sums_ready = mem.semaphore(f"{name}_sums_ready")
        self.mean_ready = mem.semaphore(f"{name}_mean_ready")
        self.centred_ready = mem.semaphore(f"{name}_centred_ready")
        self.squares_ready = mem.semaphore(f"{name}_squares_ready")
        self.sum_squares_ready = mem.semaphore(f"{name}_sum_squares_ready")
        self.variance_ready = mem.semaphore(f"{name}_variance_ready")
        self.rstd_ready = mem.semaphore(f"{name}_rstd_ready")

    def mean(self, dve, n):
        dve.wait_ge(self.y_ready, n)
        dve.tensor_reduce(self.sums[:, :], self.y[:, :, :], AX.X, ALU.add).then_inc(self.sums_ready, 1)
        dve.wait_ge(self.sums_ready, n)
        dve.tensor_scalar(self.minus_mean[:, :], self.sums[:, :], -1.0 / DIM, None, ALU.mult)\
           .then_inc(self.mean_ready, 1)

    def centre(self, pool, n):
        pool.wait_ge(self.mean_ready, n)
        pool.tensor_tensor(self.centred[:, :, :], self.y[:, :, :], over_nodes(self.minus_mean[:, :]), ALU.add)\
            .then_inc(self.centred_ready, 1)

    def square(self, act, n):
        act.wait_ge(self.centred_ready, n)
        act.activation(self.squares[:, :, :], self.centred[:, :, :], ACT.Square).then_inc(self.squares_ready, 1)

    def variance(self, dve, n):
        dve.wait_ge(self.squares_ready, n)
        dve.tensor_reduce(self.sum_squares[:, :], self.squares[:, :, :], AX.X, ALU.add)\
           .then_inc(self.sum_squares_ready, 1)
        dve.wait_ge(self.sum_squares_ready, n)
        dve.tensor_scalar(self.variances[:, :], self.sum_squares[:, :], 1.0 / DIM, EPS, ALU.mult, ALU.add)\
           .then_inc(self.variance_ready, 1)

    def inverse_deviation(self, pool, n):
        pool.wait_ge(self.variance_ready, n)
        pool.tensor_tensor(self.rstd[:, :], self.variances[:, :], self.exponent[:, :], ALU.pow)\
            .then_inc(self.rstd_ready, 1)




def setup(nc, ins, keep):
    with ExitStack() as stack:
        mem = Memory(nc, stack, "setup")
        adj = mem.sbuf("adj", [P, TILES, NODES], I32)
        rows = mem.sbuf("rows", [P, TILES, NODES])
        ones = mem.sbuf("ones", [P, P], F32R)
        degree = mem.psum("degree")
        turned = [mem.psum(f"turned{k}") for k in range(2)]
        loaded = [mem.semaphore(f"loaded{t}") for t in range(TILES)]
        degrees = mem.sbuf("degrees", [P, TILES])
        consts, masked, turned_full, copied, degree_ready, degrees_ready, empty_ready = (
            mem.semaphore(n) for n in ("consts", "masked", "turned_full", "copied", "degree_ready", "degrees_ready",
                                       "empty_ready"))
        adj_v = ins["adj"].rearrange("(t p) j -> p t j", p=P)
        with nc.Block() as block:

            @block.sync
            def _(sp):
                for t in range(TILES):
                    sp.dma_start(adj[:, t, :], adj_v[:, t, :]).then_inc(loaded[t], 16)
                sp.dma_start(keep.x[:, 0:2, :, :], x_rows(ins)[:, 0:2, :, :]).then_inc(keep.first_x_loaded, 16)

            @block.gpsimd
            def _(pool):
                pool.memset(keep.ident[:, :], 0.0).then_inc(consts, 1)
                pool.memset(keep.minus_half[:, :], -0.5).then_inc(consts, 1)
                pool.memset(ones[:, :].bitcast(F32), 1.0).then_inc(consts, 1)
                pool.memset(keep.ones[:, :], 1.0).then_inc(consts, 1)
                pool.memset(keep.x[:, BATCH, :, :], 0.0).then_inc(consts, 1)
                pool.wait_ge(consts, 5)
                pool.affine_select(out=keep.ident[:, :], in_=keep.ident[:, :], compare_op=ALU.not_equal, fill=1.0,
                                   base=0, pattern=[[-1, P]], channel_multiplier=1).then_inc(consts, 1)

            @block.vector
            def _(dve):
                for t in range(TILES):
                    dve.wait_ge(loaded[t], 16)
                    dve.tensor_scalar(rows[:, t, :], adj[:, t, :], 0.0, None, ALU.is_gt).then_inc(masked, 1)
                for t in range(TILES):
                    dve.wait_ge(masked, t + 1)
                    dve.tensor_reduce(degrees[:, t:t + 1], rows[:, t, :], AX.X, ALU.add).then_inc(degrees_ready, 1)
                dve.wait_ge(degrees_ready, TILES)
                dve.tensor_scalar(keep.no_neighbour[:, :], degrees[:, :], 0.0, 1.0 / NODES, ALU.is_equal, ALU.mult)\
                   .then_inc(empty_ready, 1)
                dve.wait_ge(degree_ready, 1)
                dve.tensor_scalar(keep.empty[:, :], degree[0:1, :], 0.0, None, ALU.is_equal).then_inc(empty_ready, 1)

            @block.tensor
            def _(pe):
                pe.wait_ge(consts, 6)
                for i in range(TILES):
                    pe.wait_ge(masked, i + 1)
                    if i >= 2:
                        pe.wait_ge(copied, i - 1)
                    for j in range(TILES):
                        last = pe.transpose(turned[i % 2][:, j * P:(j + 1) * P], rows[:, i, j * P:(j + 1) * P],
                                            keep.ident[:, :])
                    last.then_inc(turned_full, 1)
                pe.wait_ge(copied, TILES)
                for j in range(TILES):
                    for h in range(HALVES):
                        last = pe.matmul(degree[:, h * HALF:(h + 1) * HALF], ones[:, :],
                                         keep.mask[:, j, h * HALF:(h + 1) * HALF],
                                         start=(j == 0), stop=(j == TILES - 1))
                last.then_inc(degree_ready, 1)

            @block.scalar
            def _(act):
                for i in range(TILES):
                    act.wait_ge(turned_full, i + 1)
                    act.activation(keep.mask[:, :, i * P:(i + 1) * P],
                                   turned[i % 2][:, :].rearrange("j (t i) -> j t i", i=P), ACT.Copy)\
                       .then_inc(copied, 1)




def additive_layer(nc, stage, keep, w_in, a_in, x_in=None):
    with ExitStack() as stack:
        mem = Memory(nc, stack, stage)
        sb, sem = mem.sbuf, mem.semaphore
        RING = 4
        w = sb("w", [DIM, DIM])
        w_turned = sb("w_turned", [DIM, DIM])
        a_cols = sb("a_cols", [DIM, 2])
        a_wide = sb("a_wide", [DIM, P + 1])
        w_aug = sb("w_aug", [DIM, AUG])
        w_wide = sb("w_wide", [DIM, P])
        x_stage = sb("x_stage", [P, TILES + 1, DIM])
        x_turned = sb("x_turned", [DIM, NODES])
        hidden = sb("hidden", [P, TILES, AUG])
        tile_top = sb("tile_top", [P, 1])
        top_pair = sb("top_pair", [1, 2])
        tops = sb("tops", [P, 2])
        below = sb("below", [P, TILES])
        low = sb("low", [P, TILES])
        gain = [sb(f"gain{k}", [P, TILES]) for k in range(2)]
        above = sb("above", [P, NODES])
        row = [sb(f"row{k}", [P, NODES]) for k in range(2)]
        values = [sb(f"values{k}", [P, TILES, WIDE]) for k in range(2)]
        total = sb("total", [P, DIM])
        plain = sb("plain", [P, TILES, DIM])
        denominators = sb("denominators", [P, TILES])
        weights = [sb(f"weights{k}", [P, NODES]) for k in range(RING)]
        recip = sb("recip", [P, TILES])
        weighted = sb("weighted", [P, TILES, DIM])
        mixed = sb("mixed", [P, TILES, DIM])
        negated = sb("negated", [P, TILES, DIM])
        expd = sb("expd", [P, TILES, DIM])
        elu = sb("elu", [P, TILES, DIM])
        norm = LayerNorm(mem, "norm", keep.minus_half)

        ps_x = mem.psum("ps_x")
        ps_s1 = mem.psum("ps_s1")
        ps_small = mem.psum("ps_small", (P, HALF))
        ps_total = mem.psum("ps_total", (P, HALF))
        ps_out = mem.psum("ps_out")

        empty_tile = sem("empty_tile")
        loaded, w_full, w_ready, prod_full, prod_ready = (
            sem(n) for n in ("loaded", "w_full", "w_ready", "prod_full", "prod_ready"))
        staged, x_full, x_ready, tile_top_ready, s1_full, hidden_full, hidden_ready = (
            sem(n) for n in ("staged", "x_full", "x_ready", "tile_top_ready", "s1_full", "hidden_full", "hidden_ready"))
        turned_top_full, minus_top_ready, pair_ready, tops_full, top_ready, below_ready, gain_ready, low_ready, above_ready, row_ready = (
            sem(n) for n in ("turned_top_full", "minus_top_ready", "pair_ready", "tops_full", "top_ready",
                             "below_ready", "gain_ready", "low_ready",
                             "above_ready", "row_ready"))
        values_ready, totals_full, total_ready, plain_ready = (
            sem(n) for n in ("values_ready", "totals_full", "total_ready", "plain_ready"))
        weights_ready, weights_used = sem("weights_ready"), sem("weights_used")
        denominators_ready, weighted_ready = sem("denominators_ready"), sem("weighted_ready")
        recip_ready, mixed_ready, negated_ready, expd_ready, elu_ready, x_written = (
            sem(n) for n in ("recip_ready", "mixed_ready", "negated_ready", "expd_ready", "elu_ready", "x_written"))

        def tile_cols(t):
            return slice(t * WIDE, t * WIDE + AUG)

        def by_tile(psum, a, b):
            return psum[:, :].rearrange("p (t c) -> p t c", c=WIDE)[:, :, a:b]

        with nc.Block() as block:

            @block.sync
            def _(sp):
                sp.dma_start(w[:, :], w_in).then_inc(loaded, 16)
                for k in range(2):
                    sp.dma_start(a_cols[:, k:k + 1], a_in[k * DIM:(k + 1) * DIM, :]).then_inc(loaded, 16)
                if x_in is not None:
                    sp.dma_start(keep.x[:, 2:BATCH, :, :], x_in[:, 2:BATCH, :, :]).then_inc(keep.x_loaded, 16)

            @block.gpsimd
            def _(pool):
                pool.memset(x_stage[:, TILES, :], 0.0).then_inc(empty_tile, 1)
                for s in range(2):
                    pool.memset(values[s][:, :, AUG:WIDE], 0.0).then_inc(empty_tile, 1)

                def stage_x(b):
                    wait(pool, x_full, b)
                    pool.tensor_copy(x_stage[:, 0:TILES, :], keep.x[:, b, :, :]).then_inc(staged, 1)

                def scale_values(b, s):
                    pool.wait_ge(low_ready, b + 1)
                    wait(pool, weights_used, TILES * (b - 1))
                    pool.tensor_tensor(values[s][:, :, 0:DIM], hidden[:, :, 0:DIM], over_nodes(low[:, :]),
                                       ALU.mult).then_inc(values_ready, 1)
                    pool.tensor_copy(values[s][:, :, DIM:AUG], low[:, :].unsqueeze(2)).then_inc(values_ready, 1)

                def fill_plain(b):
                    pool.wait_ge(total_ready, b + 1)
                    wait(pool, mixed_ready, b)
                    pool.tensor_tensor(plain[:, :, :], over_tiles(total[:, :]), over_nodes(keep.no_neighbour[:, :]),
                                       ALU.mult).then_inc(plain_ready, 1)

                def residual(b):
                    pool.wait_ge(empty_tile, 3)
                    pool.wait_ge(elu_ready, b + 1)
                    pool.tensor_tensor(norm.y[:, :, :], elu[:, :, :], keep.x[:, b, :, :], ALU.add)\
                        .then_inc(norm.y_ready, 1)
                    norm.centre(pool, b + 1)

                def write_x(b):
                    norm.inverse_deviation(pool, b + 1)
                    pool.wait_ge(empty_tile, 3)
                    pool.wait_ge(norm.rstd_ready, b + 1)
                    pool.tensor_tensor(keep.x[:, b, :, :], norm.centred[:, :, :], over_nodes(norm.rstd[:, :]),
                                       ALU.mult).then_inc(x_written, 1)

                def step(b, s, first=False, last=False):
                    if not first:
                        residual(b - 1)
                    fill_plain(b)
                    if not last:
                        stage_x(b + 2)
                    if not first:
                        write_x(b - 1)
                    scale_values(b + 1, 1 - s)

                pool.wait_ge(keep.first_x_loaded, 16)
                stage_x(0)
                stage_x(1)
                scale_values(0, 0)
                pool.wait_ge(keep.x_loaded, 16)
                step(0, 0, first=True)
                with pool.Fori(0, (BATCH - 2) // 2) as i:
                    step(2 * i + 1, 1)
                    step(2 * i + 2, 0)
                step(BATCH - 1, 1, last=True)
                residual(BATCH - 1)
                write_x(BATCH - 1)
                pool.wait_ge(x_written, BATCH)

            @block.vector
            def _(dve):
                dve.wait_ge(loaded, 48)
                dve.tensor_copy(a_wide[:, 0:1], a_cols[:, 1:2]).then_inc(w_ready, 1)
                dve.tensor_copy(a_wide[:, 1:1 + P], a_cols[:, 0:1].to_broadcast([DIM, P])).then_inc(w_ready, 1)
                dve.wait_ge(w_full, 1)
                dve.tensor_copy(w_turned[:, :], ps_x[0:DIM, 0:DIM]).then_inc(w_ready, 1)
                dve.tensor_copy(w_aug[:, 0:DIM], w[:, :]).then_inc(w_ready, 1)
                dve.wait_ge(prod_full, 1)
                dve.tensor_copy(w_aug[:, DIM:AUG], ps_s1[0:DIM, 0:1]).then_inc(prod_ready, 1)
                dve.tensor_copy(w_wide[:, :], ps_s1[0:DIM, 1:1 + P]).then_inc(prod_ready, 1)

                def find_tile_top(b):
                    dve.wait_ge(hidden_ready, b + 1)
                    dve.tensor_reduce(tile_top[:, :], hidden[:, :, DIM:AUG].rearrange("p t c -> p (t c)"), AX.X,
                                      ALU.max).then_inc(tile_top_ready, 1)

                def find_top(b):
                    dve.wait_ge(turned_top_full, b + 1)
                    dve.tensor_reduce(top_pair[:, 0:1], ps_small[0:1, 0:P], AX.X, ALU.max, negate=True)\
                       .then_inc(minus_top_ready, 1)
                    dve.wait_ge(minus_top_ready, b + 1)
                    dve.tensor_scalar(top_pair[:, 1:2], top_pair[:, 0:1], -1.0, None, ALU.mult)\
                       .then_inc(pair_ready, 1)

                def copy_tops(b):
                    dve.wait_ge(tops_full, b + 1)
                    dve.tensor_copy(tops[:, :], ps_small[:, P:P + 2]).then_inc(top_ready, 1)

                def weigh(b, s, t):
                    if t == 0:
                        dve.wait_ge(row_ready, b + 1)
                        dve.wait_ge(gain_ready, b + 1)
                    wait(dve, weights_used, TILES * b + t - RING + 1)
                    dve.scalar_tensor_tensor(out=weights[t % RING][:, :], in0=row[s][:, :],
                                             scalar=gain[s][:, t:t + 1], in1=keep.mask[:, t, :].bitcast(F32),
                                             op0=ALU.max, op1=ALU.mult).then_inc(weights_ready, 1)

                def divide(b):
                    dve.wait_ge(weights_used, TILES * (b + 1))
                    dve.tensor_tensor(denominators[:, :].unsqueeze(2), by_tile(ps_out, DIM, AUG),
                                      keep.no_neighbour[:, :].unsqueeze(2), ALU.add).then_inc(denominators_ready, 1)
                    dve.wait_ge(denominators_ready, b + 1)
                    dve.reciprocal(recip[:, :], denominators[:, :]).then_inc(recip_ready, 1)
                    dve.wait_ge(recip_ready, b + 1)
                    dve.tensor_tensor(weighted[:, :, :], by_tile(ps_out, 0, DIM), over_nodes(recip[:, :]),
                                      ALU.mult).then_inc(weighted_ready, 1)
                    dve.wait_ge(plain_ready, b + 1)
                    dve.wait_ge(weighted_ready, b + 1)
                    wait(dve, negated_ready, b)
                    dve.tensor_tensor(mixed[:, :, :], weighted[:, :, :], plain[:, :, :], ALU.add)\
                       .then_inc(mixed_ready, 1)

                def add_totals(b):
                    dve.wait_ge(totals_full, b + 1)
                    wait(dve, plain_ready, b)
                    dve.tensor_reduce(total[:, :], ps_total[:, :].rearrange("p (t d) -> p d t", t=TILES), AX.X,
                                      ALU.add).then_inc(total_ready, 1)

                def apply_elu(b):
                    dve.wait_ge(expd_ready, b + 1)
                    dve.scalar_tensor_tensor(out=elu[:, :, :], in0=expd[:, :, :], scalar=-1.0, in1=mixed[:, :, :],
                                             op0=ALU.add, op1=ALU.max).then_inc(elu_ready, 1)

                def step(b, s, first=False):
                    weigh(b, s, 0)
                    if not first:
                        divide(b - 1)
                    weigh(b, s, 1)
                    add_totals(b)
                    if not first:
                        apply_elu(b - 1)
                    weigh(b, s, 2)
                    if not first:
                        norm.mean(dve, b)
                    weigh(b, s, 3)
                    weigh(b, s, 4)
                    find_tile_top(b + 1)
                    weigh(b, s, 5)
                    find_top(b + 1)
                    weigh(b, s, 6)
                    copy_tops(b + 1)
                    weigh(b, s, 7)
                    if not first:
                        norm.variance(dve, b)

                find_tile_top(0)
                find_top(0)
                copy_tops(0)
                step(0, 0, first=True)
                with dve.Fori(0, (BATCH - 2) // 2) as i:
                    step(2 * i + 1, 1)
                    step(2 * i + 2, 0)
                step(BATCH - 1, 1)
                divide(BATCH - 1)
                apply_elu(BATCH - 1)
                norm.mean(dve, BATCH)
                norm.variance(dve, BATCH)

            @block.scalar
            def _(act):

                def copy_x(b):
                    act.wait_ge(x_full, b + 1)
                    act.activation(x_turned[:, :], ps_x[0:DIM, :], ACT.Copy).then_inc(x_ready, 1)

                def copy_hidden(b):
                    act.wait_ge(hidden_full, b + 1)
                    wait(act, values_ready, 2 * b)
                    wait(act, totals_full, b)
                    act.activation(hidden[:, :, :], by_tile(ps_x, 0, AUG), ACT.Copy).then_inc(hidden_ready, 1)

                def factors(b, s):
                    act.wait_ge(top_ready, b + 1)
                    act.wait_ge(hidden_ready, b + 1)
                    act.activation(below[:, :], hidden[:, :, DIM:AUG].rearrange("p t c -> p (t c)"), ACT.Identity,
                                   bias=tops[:, 0:1]).then_inc(below_ready, 1)
                    act.wait_ge(s1_full, b + 1)
                    act.activation(above[:, :], ps_s1[:, :], ACT.Relu, bias=tops[:, 1:2]).then_inc(above_ready, 1)
                    act.wait_ge(below_ready, b + 1)
                    wait(act, weights_ready, TILES * (b - 1))
                    act.activation(gain[s][:, :], below[:, :], ACT.Exp, scale=1.0 - SLOPE).then_inc(gain_ready, 1)
                    act.activation(low[:, :], below[:, :], ACT.Exp, scale=SLOPE).then_inc(low_ready, 1)
                    act.wait_ge(above_ready, b + 1)
                    act.activation(row[s][:, :], above[:, :], ACT.Exp, scale=SLOPE - 1.0).then_inc(row_ready, 1)

                def exp_of_negative(b):
                    act.wait_ge(mixed_ready, b + 1)
                    act.activation(negated[:, :, :], mixed[:, :, :], ACT.Relu, scale=-1.0).then_inc(negated_ready, 1)
                    act.wait_ge(negated_ready, b + 1)
                    wait(act, elu_ready, b)
                    act.activation(expd[:, :, :], negated[:, :, :], ACT.Exp, scale=-1.0).then_inc(expd_ready, 1)

                def step(b, s, first=False):
                    if not first:
                        exp_of_negative(b - 1)
                    copy_x(b + 1)
                    copy_hidden(b + 1)
                    if not first:
                        norm.square(act, b)
                    factors(b + 1, 1 - s)

                copy_x(0)
                copy_hidden(0)
                factors(0, 0)
                step(0, 0, first=True)
                with act.Fori(0, (BATCH - 2) // 2) as i:
                    step(2 * i + 1, 1)
                    step(2 * i + 2, 0)
                step(BATCH - 1, 1)
                exp_of_negative(BATCH - 1)
                norm.square(act, BATCH)

            @block.tensor
            def _(pe):
                pe.wait_ge(loaded, 48)
                pe.transpose(ps_x[0:DIM, 0:DIM], w[:, :], keep.ident[0:DIM, 0:DIM]).then_inc(w_full, 1)
                pe.wait_ge(w_ready, 4)
                pe.matmul(ps_s1[0:DIM, 0:P + 1], w_turned[:, :], a_wide[:, :], start=True, stop=True)\
                  .then_inc(prod_full, 1)
                pe.wait_ge(prod_ready, 2)
                pe.wait_ge(empty_tile, 3)

                def turn_x(b):
                    pe.wait_ge(staged, b + 1)
                    wait(pe, hidden_ready, b)
                    for t in range(TILES):
                        last = pe.transpose(ps_x[:, t * P:(t + 1) * P],
                                            x_stage[:, t:t + 2, :].rearrange("p t c -> p (t c)"), keep.ident[:, :])
                    last.then_inc(x_full, 1)

                def project(b):
                    pe.wait_ge(x_ready, b + 1)
                    for t in range(TILES):
                        last = pe.matmul(ps_x[:, tile_cols(t)], x_turned[:, t * P:(t + 1) * P], w_aug[:, :],
                                         start=True, stop=True)
                    last.then_inc(hidden_full, 1)
                    wait(pe, above_ready, b)
                    for h in range(HALVES):
                        last = pe.matmul(ps_s1[:, h * HALF:(h + 1) * HALF], w_wide[:, 0:P],
                                         x_turned[:, h * HALF:(h + 1) * HALF], start=True, stop=True)
                    last.then_inc(s1_full, 1)

                def turn_top(b):
                    pe.wait_ge(tile_top_ready, b + 1)
                    wait(pe, top_ready, b)
                    pe.matmul(ps_small[0:1, 0:P], tile_top[:, :], keep.ident[:, :], start=True, stop=True)\
                      .then_inc(turned_top_full, 1)

                def spread_tops(b):
                    pe.wait_ge(pair_ready, b + 1)
                    pe.matmul(ps_small[:, P:P + 2], keep.ones[0:1, :], top_pair[:, :], start=True, stop=True)\
                      .then_inc(tops_full, 1)

                def sum_up(b):
                    pe.wait_ge(hidden_ready, b + 1)
                    wait(pe, total_ready, b)
                    pe.matmul(ps_total[:, :], keep.ones[:, :], hidden[:, :, 0:DIM], start=True, stop=True)\
                      .then_inc(totals_full, 1)

                def multiply(b, s, t):
                    if t == 0:
                        pe.wait_ge(values_ready, 2 * (b + 1))
                        wait(pe, weighted_ready, b)
                    pe.wait_ge(weights_ready, TILES * b + t + 1)
                    for i in range(TILES):
                        last = pe.matmul(ps_out[:, i * WIDE:(i + 1) * WIDE], weights[t % RING][:, i * P:(i + 1) * P],
                                         values[s][:, t, :], start=(t == 0 and i % PER_BANK == 0),
                                         stop=(t == TILES - 1),
                                         skip_group_check=True)
                    last.then_inc(weights_used, 1)

                def step(b, s):
                    turn_x(b + 1)
                    multiply(b, s, 0)
                    multiply(b, s, 1)
                    project(b + 1)
                    for t in range(2, TILES):
                        multiply(b, s, t)
                        if t == 2:
                            turn_top(b + 1)
                        if t == 3:
                            spread_tops(b + 1)
                    sum_up(b + 1)

                turn_x(0)
                project(0)
                turn_top(0)
                spread_tops(0)
                sum_up(0)
                step(0, 0)
                with pe.Fori(0, (BATCH - 2) // 2) as i:
                    step(2 * i + 1, 1)
                    step(2 * i + 2, 0)
                step(BATCH - 1, 1)




def dot_layer(nc, stage, keep, ins, out):
    with ExitStack() as stack:
        mem = Memory(nc, stack, stage)
        sb, sem = mem.sbuf, mem.semaphore
        RING = 4
        LAG = 2
        UNITS = HEADS + 1
        CAT = HEADS * DIM
        SLOTS = 3

        wh_in = sb("wh_in", [P, 2, 2, DIM])
        wo_in = sb("wo_in", [DIM, CAT])
        wh_high = sb("wh_high", [P, CAT], F32R)
        wh_parts = sb("wh_parts", [P, HEADS, P], F32R)
        wo_twice = sb("wo_twice", [P, 2, P])
        sum_parts = sb("sum_parts", [P, DIM], F32R)
        rows_in = sb("rows_in", [P, 3, DIM])
        bh = sb("bh", [P, HEADS, DIM])
        minus_high = sb("minus_high", [P, 1])
        minus_sum = sb("minus_sum", [DIM, P], F32R)

        x_stage = sb("x_stage", [P, TILES, 2, DIM])
        x_high = sb("x_high", [P, NODES], F32R)
        x_low = sb("x_low", [P, NODES], F32R)
        high_high = [sb(f"high_high{k}", [P, NODES], F32R) for k in range(SLOTS)]
        low_high = [sb(f"low_high{k}", [P, NODES], F32R) for k in range(SLOTS)]
        high_one = [sb(f"high_one{k}", [AUG, NODES], F32R) for k in range(SLOTS)]
        low_norm = [sb(f"low_norm{k}", [AUG, NODES], F32R) for k in range(SLOTS)]
        values = [sb(f"values{k}", [P, TILES, WIDE]) for k in range(SLOTS)]
        squares = sb("squares", [DIM, NODES], F32R)
        weights = [sb(f"weights{k}", [P, NODES]) for k in range(RING)]
        recip = sb("recip", [P, TILES])
        mixed = sb("mixed", [P, TILES, DIM])
        biased = sb("biased", [P, TILES, DIM])
        cat = sb("cat", [P, TILES, CAT])
        cat_turned = sb("cat_turned", [P, 2, NODES])
        inner = LayerNorm(mem, "inner", keep.minus_half)
        outer = LayerNorm(mem, "outer", keep.minus_half)
        normed = sb("normed", [P, TILES, DIM])
        gained = outer.centred
        shifted = normed

        ps_scores = [mem.psum(f"ps_scores{k}") for k in range(2)]
        ps_out = mem.psum("ps_out")
        ps_prep = mem.psum("ps_prep")

        loaded, set_up, turned_full, wh_rounded, turned_ready = (
            sem(n) for n in ("loaded", "set_up", "turned_full", "wh_rounded", "turned_ready"))
        staged, x_full, x_high_ready, x_low_ready, cat_ready, cat_full, cat_turned_ready = (
            sem(n) for n in ("staged", "x_full", "x_high_ready", "x_low_ready", "cat_ready", "cat_full",
                             "cat_turned_ready"))
        hidden_full, norm_full, values_full = sem("hidden_full"), sem("norm_full"), sem("values_full")
        high_ready, low_ready, low_copied, high_copied, squares_ready, norm_ready, values_ready = (
            sem(n) for n in ("high_ready", "low_ready", "low_copied", "high_copied", "squares_ready", "norm_ready",
                             "values_ready"))
        scores_full, exp_ready, weights_ready, weights_used = (
            sem(n) for n in ("scores_full", "exp_ready", "weights_ready", "weights_used"))
        recip_ready, mixed_ready, biased_ready = (sem(n) for n in ("recip_ready", "mixed_ready", "biased_ready"))
        normed_ready, gained_ready, shifted_ready, x_written, stored = (
            sem(n) for n in ("normed_ready", "gained_ready", "shifted_ready", "x_written", "stored"))

        SECOND = HEADS
        SLOT = (0, 1, 0, 1, 2)
        HIDDEN_AT, HIGH_AT, LOW_AT, NORMS_AT, VALUES_AT = 2, 3, 4, 5, 6

        def order(first):
            return (0, 1, 2, 3) if first else (0, 1, SECOND, 2, 3)

        def first_unit(b):
            return 0 if isinstance(b, int) and b == 0 else UNITS * b - 1

        class Step:

            def __init__(self, b, first=False, last=False):
                self.b, self.first, self.last = b, first, last
                self.kinds, self.unit0 = order(first), first_unit(b)

            def before(self, k):
                return self.kinds[k - 1] if k else HEADS - 1

            def after(self, k):
                return self.kinds[k + 1] if k + 1 < len(self.kinds) else 0

            def closes(self, k):
                return k + 1 == len(self.kinds)

            def turns_x(self, k):
                return not self.last and k + 2 == len(self.kinds)

        def run_all(engine, run):
            run(Step(0, first=True))
            with engine.Fori(1, BATCH - 1) as b:
                run(Step(b))
            run(Step(BATCH - 1, last=True))

        def final_unit():
            return first_unit(BATCH)

        with nc.Block() as block:

            @block.sync
            def _(sp):
                for g in range(2):
                    for copy in range(2):
                        sp.dma_start(wh_in[:, g, copy, :], ins["L3_gnn_Wh"][2 * g:2 * g + 2, :, :]
                                     .rearrange("h d c -> (h d) c")).then_inc(loaded, 16)
                sp.dma_start(wo_in[:, :], ins["L3_gnn_Wo"]).then_inc(loaded, 16)
                for h in range(HEADS):
                    sp.dma_start(bh[:, h, :], ins["L3_gnn_bh"][h:h + 1, :].to_broadcast([P, DIM])).then_inc(loaded, 16)
                for k, name in enumerate(("L3_gnn_bo", "L3_gnn_gamma", "L3_gnn_beta")):
                    sp.dma_start(rows_in[:, k, :], ins[name].unsqueeze(0).to_broadcast([P, DIM])).then_inc(loaded, 16)
                out_v = out.rearrange("b (t p) d -> p b t d", p=P)
                with sp.Fori(0, BATCH) as b:
                    sp.wait_ge(x_written, b + 1)
                    sp.dma_start(out_v[:, b, :, :], keep.x[:, b, :, :]).then_inc(stored, 16)
                sp.wait_ge(stored, 16 * BATCH)

            @block.gpsimd
            def _(pool):
                pool.memset(minus_high[:, :], -1.0).then_inc(set_up, 1)
                pool.wait_ge(set_up, 1)
                pool.memset(minus_high[DIM:P, :], 0.0).then_inc(set_up, 1)
                pool.wait_ge(set_up, 2)
                pool.memset(minus_sum[:, :].bitcast(F32), 0.0).then_inc(set_up, 1)
                pool.wait_ge(set_up, 3)
                pool.memset(minus_sum[:, DIM:AUG].bitcast(F32), -1.0).then_inc(set_up, 1)
                for s in range(SLOTS):
                    pool.wait_ge(set_up, 4 + 3 * s)
                    pool.memset(high_one[s][DIM:AUG, :].bitcast(F32), 1.0).then_inc(set_up, 1)
                    pool.wait_ge(set_up, 5 + 3 * s)
                    pool.memset(values[s][:, :, DIM:AUG], 1.0).then_inc(set_up, 1)
                    pool.memset(values[s][:, :, AUG:WIDE], 0.0).then_inc(set_up, 1)
                pool.wait_ge(loaded, 16 * (5 + HEADS + 3))

                def stage_x(b):
                    pool.wait_ge(set_up, 1)
                    wait(pool, x_high_ready, b)
                    pool.tensor_copy(x_stage[:, :, :, :], keep.x[:, b, :, :].unsqueeze(2)
                                     .to_broadcast([P, TILES, 2, DIM])).then_inc(staged, 1)

                def copy_high(u, s):
                    pool.wait_ge(high_ready, u + 1)
                    pool.tensor_tensor(high_one[s][0:DIM, :], high_high[s][0:DIM, :].bitcast(F32),
                                       keep.ones[0:DIM, 0:1].to_broadcast([DIM, NODES]), ALU.mult)\
                        .then_inc(high_copied, 1)

                def add_bias(u, kind):
                    pool.wait_ge(mixed_ready, u + 1)
                    row = rows_in[:, 0, :] if kind == SECOND else bh[:, kind, :]
                    pool.tensor_tensor(biased[:, :, :], mixed[:, :, :], over_tiles(row), ALU.add)\
                        .then_inc(biased_ready, 1)

                def inner_affine(n):
                    inner.inverse_deviation(pool, n)
                    pool.wait_ge(inner.rstd_ready, n)
                    pool.tensor_tensor(normed[:, :, :], inner.centred[:, :, :], over_nodes(inner.rstd[:, :]), ALU.mult)\
                        .then_inc(normed_ready, 1)
                    pool.wait_ge(normed_ready, n)
                    pool.tensor_tensor(gained[:, :, :], normed[:, :, :], over_tiles(rows_in[:, 1, :]), ALU.mult)\
                        .then_inc(gained_ready, 1)
                    pool.wait_ge(gained_ready, n)
                    pool.tensor_tensor(shifted[:, :, :], gained[:, :, :], over_tiles(rows_in[:, 2, :]), ALU.add)\
                        .then_inc(shifted_ready, 1)
                    pool.wait_ge(set_up, 1)
                    pool.wait_ge(shifted_ready, n)
                    pool.tensor_tensor(outer.y[:, :, :], shifted[:, :, :], keep.x[:, n - 1, :, :], ALU.add)\
                        .then_inc(outer.y_ready, 1)
                    outer.centre(pool, n)

                def write_x(n):
                    outer.inverse_deviation(pool, n)
                    pool.wait_ge(set_up, 1)
                    pool.wait_ge(outer.rstd_ready, n)
                    pool.tensor_tensor(keep.x[:, n - 1, :, :], outer.centred[:, :, :], over_nodes(outer.rstd[:, :]),
                                       ALU.mult).then_inc(x_written, 1)

                def run(st):
                    for k, kind in enumerate(st.kinds):
                        u = st.unit0 + k
                        if k == 0 and not st.last:
                            stage_x(st.b + 1)
                        if not (st.first and k == 0):
                            add_bias(u - 1, st.before(k))
                        if not (st.last and st.closes(k)):
                            copy_high(u + 1, SLOT[st.after(k)])
                        if not st.first and k == 3:
                            inner.centre(pool, st.b)
                        if not st.first and k == 4:
                            inner_affine(st.b)
                            write_x(st.b)

                stage_x(0)
                copy_high(0, SLOT[0])
                run_all(pool, run)
                u = final_unit()
                add_bias(u - 1, HEADS - 1)
                copy_high(u, SLOT[SECOND])
                add_bias(u, SECOND)
                inner.centre(pool, BATCH)
                inner_affine(BATCH)
                write_x(BATCH)
                pool.wait_ge(x_written, BATCH)

            @block.vector
            def _(dve):
                dve.wait_ge(wh_rounded, 1)
                for copy in range(2):
                    to, heads = slice(copy * DIM, (copy + 1) * DIM), "c (h d) -> c h d"
                    dve.tensor_copy(wh_parts[0:DIM, :, to],
                                    wh_high[0:DIM, :].bitcast(F32).rearrange(heads, h=HEADS))\
                       .then_inc(turned_ready, 1)
                    dve.scalar_tensor_tensor(out=wh_parts[DIM:P, :, to],
                                             in0=wh_high[DIM:P, :].bitcast(F32).rearrange(heads, h=HEADS), scalar=-1.0,
                                             in1=ps_prep[DIM:P, 0:CAT].rearrange(heads, h=HEADS),
                                             op0=ALU.mult, op1=ALU.add).then_inc(turned_ready, 1)
                    dve.tensor_copy(wo_twice[:, :, to],
                                    ps_prep[:, HALF:HALF + 2 * DIM].rearrange("k (c d) -> k c d", c=2))\
                       .then_inc(turned_ready, 1)
                dve.tensor_tensor(sum_parts[:, :], keep.ident[:, 0:DIM], keep.ident[:, DIM:P], ALU.add)\
                   .then_inc(turned_ready, 1)
                for t in range(TILES):
                    dve.tensor_tensor(keep.mask[:, t, t * P:(t + 1) * P],
                                      keep.mask[:, t, t * P:(t + 1) * P].bitcast(F32), keep.ident[:, :], ALU.max)\
                       .then_inc(turned_ready, 1)
                dve.wait_ge(turned_ready, 7 + TILES)
                dve.wait_ge(set_up, 4 + 3 * SLOTS)

                def split_low(u, s):
                    dve.wait_ge(squares_ready, u + 1)
                    dve.scalar_tensor_tensor(out=low_high[s][:, :], in0=high_high[s][:, :].bitcast(F32),
                                             scalar=minus_high[:, 0:1], in1=ps_prep[:, :], op0=ALU.mult, op1=ALU.add)\
                       .then_inc(low_ready, 1)

                def lower_x(b):
                    dve.wait_ge(x_high_ready, b + 1)
                    dve.scalar_tensor_tensor(out=x_low[:, :], in0=x_high[:, :].bitcast(F32), scalar=-1.0,
                                             in1=ps_prep[:, :], op0=ALU.mult, op1=ALU.add).then_inc(x_low_ready, 1)

                def copy_low(u, s):
                    dve.wait_ge(low_ready, u + 1)
                    dve.tensor_copy(low_norm[s][0:DIM, :], low_high[s][0:DIM, :].bitcast(F32))\
                       .then_inc(low_copied, 1)

                def mask(u, t):
                    dve.wait_ge(exp_ready, TILES * u + t + 1)
                    buf = weights[t % RING]
                    dve.tensor_tensor(buf[:, :], buf[:, :], keep.mask[:, t, :].bitcast(F32), ALU.mult)\
                       .then_inc(weights_ready, 1)

                def divide(u):
                    out = ps_out[:, :].rearrange("p (t c) -> p t c", c=WIDE)
                    dve.wait_ge(weights_used, TILES * (u + 1))
                    dve.reciprocal(recip[:, :].unsqueeze(2), out[:, :, DIM:AUG]).then_inc(recip_ready, 1)
                    dve.wait_ge(recip_ready, u + 1)
                    wait(dve, biased_ready, u)
                    dve.tensor_tensor(mixed[:, :, :], out[:, :, 0:DIM], over_nodes(recip[:, :]), ALU.mult)\
                       .then_inc(mixed_ready, 1)

                def leaky(u, kind):
                    dve.wait_ge(biased_ready, u + 1)
                    to = inner.y[:, :, :] if kind == SECOND else cat[:, :, kind * DIM:(kind + 1) * DIM]
                    dve.scalar_tensor_tensor(out=to, in0=biased[:, :, :], scalar=SLOPE, in1=biased[:, :, :],
                                             op0=ALU.mult, op1=ALU.max)\
                       .then_inc(inner.y_ready if kind == SECOND else cat_ready, 1)

                def run(st):
                    for k, kind in enumerate(st.kinds):
                        u, s = st.unit0 + k, SLOT[st.after(k)]
                        for t in range(TILES):
                            if t == LOW_AT and not (st.last and st.closes(k)):
                                split_low(u + 1, s)
                            mask(u, t)
                            if t == LAG - 1 and not (st.first and k == 0):
                                divide(u - 1)
                            if t == 2 and not (st.first and k == 0):
                                leaky(u - 1, st.before(k))
                            if t == LOW_AT and not (st.last and st.closes(k)):
                                copy_low(u + 1, s)
                            if not st.last and st.closes(k) and t == 0:
                                lower_x(st.b + 1)
                            if not st.first and (k, t) == (3, 4):
                                inner.mean(dve, st.b)
                            if not st.first and (k, t) == (3, 7):
                                inner.variance(dve, st.b)
                            if not st.first and (k, t) == (4, 6):
                                outer.mean(dve, st.b)
                            if not st.first and (k, t) == (4, 7):
                                outer.variance(dve, st.b)

                lower_x(0)
                split_low(0, SLOT[0])
                copy_low(0, SLOT[0])
                run_all(dve, run)
                u = final_unit()
                divide(u - 1)
                leaky(u - 1, HEADS - 1)
                split_low(u, SLOT[SECOND])
                copy_low(u, SLOT[SECOND])
                for t in range(TILES):
                    mask(u, t)
                divide(u)
                leaky(u, SECOND)
                inner.mean(dve, BATCH)
                inner.variance(dve, BATCH)
                outer.mean(dve, BATCH)
                outer.variance(dve, BATCH)

            @block.scalar
            def _(act):
                act.wait_ge(turned_full, 1)
                act.activation(wh_high[:, :], ps_prep[:, 0:CAT], ACT.Copy).then_inc(wh_rounded, 1)

                def round_x(b):
                    act.wait_ge(x_full, b + 1)
                    act.activation(x_high[:, :], ps_prep[:, :], ACT.Copy).then_inc(x_high_ready, 1)

                def round_high(u, s):
                    act.wait_ge(hidden_full, u + 1)
                    act.activation(high_high[s][:, :], ps_prep[:, :], ACT.Copy).then_inc(high_ready, 1)

                def square(u):
                    act.wait_ge(hidden_full, u + 1)
                    act.activation(squares[:, :], ps_prep[0:DIM, :], ACT.Square).then_inc(squares_ready, 1)

                def copy_norm(u, s):
                    act.wait_ge(norm_full, u + 1)
                    act.activation(low_norm[s][DIM:AUG, :], ps_prep[DIM:AUG, :], ACT.Copy).then_inc(norm_ready, 1)

                def copy_values(u, s):
                    act.wait_ge(values_full, u + 1)
                    act.activation(values[s][:, :, 0:DIM], ps_prep[:, 0:HALF].rearrange("p (t d) -> p t d", d=DIM),
                                   ACT.Copy).then_inc(values_ready, 1)

                def copy_cat(b, c):
                    act.wait_ge(cat_full, 2 * b + c + 1)
                    act.activation(cat_turned[:, c, :], ps_prep[:, :], ACT.Copy).then_inc(cat_turned_ready, 1)

                def exp(u, t):
                    act.wait_ge(scores_full, TILES * u + t + 1)
                    wait(act, weights_used, TILES * u + t + 1 - RING)
                    act.activation(weights[t % RING][:, :], ps_scores[t % 2][:, :], ACT.Exp).then_inc(exp_ready, 1)

                def run(st):
                    for k, kind in enumerate(st.kinds):
                        u, s = st.unit0 + k, SLOT[st.after(k)]
                        for t in range(TILES):
                            exp(u, t)
                            if st.turns_x(k) and t == TILES - 1:
                                round_x(st.b + 1)
                            if not (st.last and st.closes(k)):
                                if t == HIGH_AT:
                                    round_high(u + 1, s)
                                    square(u + 1)
                                if t == NORMS_AT:
                                    copy_norm(u + 1, s)
                                if t == VALUES_AT:
                                    copy_values(u + 1, s)
                            if not st.first and (k, t) in ((0, TILES - 1), (1, 0)):
                                copy_cat(st.b - 1, k)
                            if not st.first and (k, t) == (3, 6):
                                inner.square(act, st.b)
                            if not st.first and (k, t) == (4, 7):
                                outer.square(act, st.b)

                round_x(0)
                round_high(0, SLOT[0])
                square(0)
                copy_norm(0, SLOT[0])
                copy_values(0, SLOT[0])
                run_all(act, run)
                u, s = final_unit(), SLOT[SECOND]
                copy_cat(BATCH - 1, 0)
                copy_cat(BATCH - 1, 1)
                round_high(u, s)
                square(u)
                copy_norm(u, s)
                copy_values(u, s)
                for t in range(TILES):
                    exp(u, t)
                inner.square(act, BATCH)
                outer.square(act, BATCH)

            @block.tensor
            def _(pe):
                pe.wait_ge(loaded, 16 * (5 + HEADS + 3))
                for g in range(2):
                    pe.transpose(ps_prep[:, g * P:(g + 1) * P], wh_in[:, g, :, :].rearrange("p k c -> p (k c)"),
                                 keep.ident[:, :])
                for c in range(2):
                    last = pe.transpose(ps_prep[:, HALF + c * DIM:HALF + (c + 1) * DIM], wo_in[:, c * P:(c + 1) * P],
                                        keep.ident[0:DIM, 0:DIM])
                last.then_inc(turned_full, 1)
                pe.wait_ge(turned_ready, 7 + TILES)
                pe.wait_ge(set_up, 4 + 3 * SLOTS)

                def turn_x(b, made):
                    pe.wait_ge(staged, b + 1)
                    wait(pe, values_ready, made)
                    for t in range(TILES):
                        last = pe.transpose(ps_prep[:, t * P:(t + 1) * P],
                                            x_stage[:, t, :, :].rearrange("p k c -> p (k c)"), keep.ident[:, :])
                    last.then_inc(x_full, 1)

                def turn_cat(b, c, made):
                    pe.wait_ge(cat_ready, HEADS * b + 2 * (c + 1))
                    if c == 0:
                        pe.wait_ge(values_ready, made)
                    else:
                        pe.wait_ge(cat_turned_ready, 2 * b + 1)
                    for t in range(TILES):
                        last = pe.transpose(ps_prep[:, t * P:(t + 1) * P], cat[:, t, c * P:(c + 1) * P],
                                            keep.ident[:, :])
                    last.then_inc(cat_full, 1)

                def hidden(u, kind, b):
                    if kind == SECOND:
                        pe.wait_ge(cat_turned_ready, 2 * (b + 1))
                    else:
                        pe.wait_ge(x_low_ready, b + 1)
                        wait(pe, values_ready, u)
                    for h in range(HALVES):
                        cols = slice(h * HALF, (h + 1) * HALF)
                        if kind == SECOND:
                            for c in range(2):
                                last = pe.matmul(ps_prep[:, cols], wo_twice[:, c, :], cat_turned[:, c, cols],
                                                 start=(c == 0), stop=(c == 1))
                        else:
                            pe.matmul(ps_prep[:, cols], wh_parts[:, kind, :], x_high[:, cols],
                                      start=True, stop=False)
                            last = pe.matmul(ps_prep[:, cols], wh_parts[:, kind, :], x_low[:, cols],
                                             start=False, stop=True)
                    last.then_inc(hidden_full, 1)

                def norms(u):
                    pe.wait_ge(squares_ready, u + 1)
                    pe.wait_ge(low_ready, u + 1)
                    for h in range(HALVES):
                        cols = slice(h * HALF, (h + 1) * HALF)
                        last = pe.matmul(ps_prep[:, cols], minus_sum[:, :], squares[:, cols], start=True, stop=True)
                    last.then_inc(norm_full, 1)

                def value_rows(u, s):
                    pe.wait_ge(norm_ready, u + 1)
                    for t in range(TILES):
                        last = pe.matmul(ps_prep[:, t * DIM:(t + 1) * DIM], low_high[s][:, t * P:(t + 1) * P],
                                         sum_parts[:, :], start=True, stop=True)
                    last.then_inc(values_full, 1)

                def scores(u, s, t):
                    if t == 0:
                        pe.wait_ge(low_copied, u + 1)
                        pe.wait_ge(high_copied, u + 1)
                        pe.wait_ge(norm_ready, u + 1)
                    wait(pe, exp_ready, TILES * u + t - 1)
                    nodes = slice(t * P, (t + 1) * P)
                    for h in range(HALVES):
                        cols = slice(h * HALF, (h + 1) * HALF)
                        pe.matmul(ps_scores[t % 2][:, cols], low_high[s][:, nodes], high_high[s][:, cols],
                                  start=True, stop=False)
                        last = pe.matmul(ps_scores[t % 2][:, cols], high_one[s][:, nodes], low_norm[s][:, cols],
                                         start=False, stop=True)
                    last.then_inc(scores_full, 1)

                def multiply(u, s, t):
                    if t == 0:
                        pe.wait_ge(values_ready, u + 1)
                        wait(pe, mixed_ready, u)
                    pe.wait_ge(weights_ready, TILES * u + t + 1)
                    for i in range(TILES):
                        last = pe.matmul(ps_out[:, i * WIDE:(i + 1) * WIDE], weights[t % RING][:, i * P:(i + 1) * P],
                                         values[s][:, t, :], start=(t == 0 and i % PER_BANK == 0),
                                         stop=(t == TILES - 1), skip_group_check=True)
                    last.then_inc(weights_used, 1)

                def run(st):
                    for k, kind in enumerate(st.kinds):
                        u, after = st.unit0 + k, st.after(k)
                        batch = st.b + 1 if st.closes(k) else st.b - 1 if after == SECOND else st.b
                        for t in range(TILES):
                            scores(u, SLOT[kind], t)
                            if not (st.last and st.closes(k)):
                                if t == HIDDEN_AT:
                                    hidden(u + 1, after, batch)
                                if t == NORMS_AT:
                                    norms(u + 1)
                                if t == VALUES_AT:
                                    value_rows(u + 1, SLOT[after])
                            if st.turns_x(k) and t == TILES - 1:
                                turn_x(st.b + 1, u + 2)
                            if not st.first and (k, t) in ((0, TILES - 1), (1, 0)):
                                turn_cat(st.b - 1, k, u + 2)
                            if t >= LAG:
                                multiply(u, SLOT[kind], t - LAG)
                            elif not (st.first and k == 0):
                                multiply(u - 1, SLOT[st.before(k)], TILES + t - LAG)

                turn_x(0, 0)
                hidden(0, 0, 0)
                norms(0)
                value_rows(0, SLOT[0])
                run_all(pe, run)
                u, s = final_unit(), SLOT[SECOND]
                for t in range(TILES - LAG, TILES):
                    multiply(u - 1, SLOT[HEADS - 1], t)
                turn_cat(BATCH - 1, 0, u)
                turn_cat(BATCH - 1, 1, u)
                hidden(u, SECOND, BATCH - 1)
                norms(u)
                value_rows(u, s)
                for t in range(TILES + LAG):
                    if t < TILES:
                        scores(u, s, t)
                    if t >= LAG:
                        multiply(u, s, t - LAG)




def feature_layer(nc, stage, keep, ins):
    with ExitStack() as stack:
        mem = Memory(nc, stack, stage)
        sb, sem = mem.sbuf, mem.semaphore
        BOTH = 2 * DIM
        BANK_TILES = HALF // (2 * BOTH)
        BANKS = TILES // BANK_TILES
        scalars = sb("scalars", [P, 3])
        rows_in = sb("rows_in", [P, 2, DIM])
        scaled = sb("scaled", [P, TILES, DIM])
        positive = [sb(f"positive{k}", [P, TILES, DIM]) for k in range(2)]
        decayed = sb("decayed", [P, TILES, DIM])
        soft = [sb(f"soft{k}", [P, TILES, DIM]) for k in range(2)]
        feat = [sb(f"feat{k}", [P, TILES, DIM]) for k in range(2)]
        product = sb("product", [P, TILES, DIM])
        score = sb("score", [P, TILES, DIM])
        tile_top = sb("tile_top", [P, DIM])
        top = sb("top", [DIM, 1])
        top_diag = sb("top_diag", [DIM, DIM])
        shifted = sb("shifted", [P, TILES, DIM])
        exact = sb("exact", [P, TILES, BOTH])
        parts = [sb(f"parts{k}", [P, TILES, 2, BOTH], F32R) for k in range(2)]
        rest_sums = sb("rest_sums", [P, TILES, BOTH])
        sums = sb("sums", [P, TILES, BOTH])
        totals = sb("totals", [1, BOTH])
        recip = sb("recip", [P, TILES, DIM])
        mixed = sb("mixed", [P, TILES, DIM])
        norm = LayerNorm(mem, "norm", keep.minus_half)

        ps_top = mem.psum("ps_top", (P, HALF))
        ps_wide = mem.psum("ps_wide", (P, HALF))
        ps_total = mem.psum("ps_total", (P, HALF))
        ps_out = [mem.psum(f"ps_out{k}", (P, HALF)) for k in range(BANKS)]

        loaded, scale_ready = sem("loaded"), sem("scale_ready")
        scaled_ready, positive_ready, decayed_ready, soft_ready = (
            sem(n) for n in ("scaled_ready", "positive_ready", "decayed_ready", "soft_ready"))
        feat_ready, product_ready, score_ready, tile_top_ready, top_full, top_ready, diag_ready, wide_full = (
            sem(n) for n in ("feat_ready", "product_ready", "score_ready", "tile_top_ready", "top_full", "top_ready",
                             "diag_ready", "wide_full"))
        shifted_ready, exp_ready, exact_ready, high_ready, rest_ready = (
            sem(n) for n in ("shifted_ready", "exp_ready", "exact_ready", "high_ready", "rest_ready"))
        total_full, totals_ready, out_full, rest_copied, sums_ready, recip_ready, mixed_ready, x_written = (
            sem(n) for n in ("total_full", "totals_ready", "out_full", "rest_copied", "sums_ready", "recip_ready",
                             "mixed_ready", "x_written"))

        def bank_tiles(k):
            return slice(k * BANK_TILES, (k + 1) * BANK_TILES)

        def out_part(k, part):
            return ps_out[k][:, :].rearrange("p (t s c) -> p t s c", s=2, c=BOTH)[:, :, part, :]

        def run_all(engine, step):
            step(0, 0)
            with engine.Fori(0, (BATCH - 4) // 2) as i:
                step(2 * i + 1, 1)
                step(2 * i + 2, 0)
            for b in range(BATCH - 3, BATCH):
                step(b, b % 2)

        def has(b):
            return not isinstance(b, int) or 0 <= b < BATCH

        with nc.Block() as block:

            @block.sync
            def _(sp):
                sp.dma_start(scalars[:, 0:1], ins["L1_gnn_w0"].to_broadcast([P, 1])).then_inc(loaded, 16)
                sp.dma_start(scalars[:, 1:2], ins["L1_gnn_b0"].unsqueeze(0).to_broadcast([P, 1]))\
                  .then_inc(loaded, 16)
                sp.dma_start(rows_in[:, 0, :], ins["L1_gnn_wa"].unsqueeze(0).to_broadcast([P, DIM]))\
                  .then_inc(loaded, 16)
                sp.dma_start(rows_in[:, 1, :], ins["L1_gnn_ba"].unsqueeze(0).to_broadcast([P, DIM]))\
                  .then_inc(loaded, 16)

            @block.gpsimd
            def _(pool):
                pool.memset(totals[:, DIM:BOTH], float(NODES)).then_inc(totals_ready, 1)
                pool.wait_ge(loaded, 64)

                def score_nodes(b, s):
                    pool.wait_ge(soft_ready, b + 1)
                    wait(pool, total_full, b - 1)
                    pool.tensor_tensor(feat[s][:, :, :], positive[s][:, :, :], soft[s][:, :, :], ALU.add)\
                        .then_inc(feat_ready, 1)
                    pool.wait_ge(feat_ready, b + 1)
                    pool.tensor_tensor(product[:, :, :], feat[s][:, :, :], over_tiles(rows_in[:, 0, :]), ALU.mult)\
                        .then_inc(product_ready, 1)
                    wait(pool, shifted_ready, b)
                    pool.wait_ge(product_ready, b + 1)
                    pool.tensor_tensor(score[:, :, :], product[:, :, :], over_tiles(rows_in[:, 1, :]), ALU.add)\
                        .then_inc(score_ready, 1)

                def weigh_feat(b, s):
                    pool.wait_ge(exp_ready, b + 1)
                    wait(pool, rest_ready, b)
                    pool.tensor_tensor(exact[:, :, 0:DIM], exact[:, :, DIM:BOTH], feat[s][:, :, :], ALU.mult)\
                        .then_inc(exact_ready, 1)

                def residual(b):
                    pool.wait_ge(totals_ready, 1)
                    pool.wait_ge(mixed_ready, BANKS * (b + 1))
                    pool.tensor_tensor(norm.y[:, :, :], mixed[:, :, :], keep.x[:, b, :, :], ALU.add)\
                        .then_inc(norm.y_ready, 1)
                    norm.centre(pool, b + 1)

                def write_x(b):
                    norm.inverse_deviation(pool, b + 1)
                    pool.wait_ge(totals_ready, 1)
                    pool.wait_ge(norm.rstd_ready, b + 1)
                    pool.tensor_tensor(keep.x[:, b, :, :], norm.centred[:, :, :], over_nodes(norm.rstd[:, :]),
                                       ALU.mult).then_inc(x_written, 1)

                def step(b, s):
                    if has(b - 1):
                        residual(b - 1)
                    if has(b + 1):
                        weigh_feat(b + 1, 1 - s)
                    if has(b + 2):
                        score_nodes(b + 2, s)
                    if has(b - 1):
                        write_x(b - 1)

                score_nodes(0, 0)
                weigh_feat(0, 0)
                score_nodes(1, 1)
                run_all(pool, step)
                residual(BATCH - 1)
                write_x(BATCH - 1)
                pool.wait_ge(x_written, BATCH)

            @block.vector
            def _(dve):
                dve.wait_ge(loaded, 64)
                dve.tensor_scalar(scalars[:, 2:3], scalars[:, 0:1], INV_SQRT2, None, ALU.mult)\
                   .then_inc(scale_ready, 1)

                def find_tile_top(b):
                    dve.wait_ge(score_ready, b + 1)
                    dve.tensor_reduce(tile_top[:, :], score[:, :, :].rearrange("p t d -> p d t"), AX.X, ALU.max)\
                       .then_inc(tile_top_ready, 1)

                def find_top(b):
                    dve.wait_ge(top_full, b + 1)
                    dve.tensor_reduce(top[:, :], ps_top[0:DIM, 0:P], AX.X, ALU.max).then_inc(top_ready, 1)
                    dve.wait_ge(top_ready, b + 1)
                    dve.tensor_scalar(top_diag[:, :], keep.ident[0:DIM, 0:DIM], top[:, 0:1], None, ALU.mult)\
                       .then_inc(diag_ready, 1)

                def shift(b):
                    dve.wait_ge(wide_full, b + 1)
                    wait(dve, exp_ready, b)
                    dve.tensor_tensor(shifted[:, :, :], score[:, :, :], over_tiles(ps_wide[:, 0:DIM]), ALU.subtract)\
                       .then_inc(shifted_ready, 1)

                def split(b, s):
                    dve.wait_ge(exact_ready, b + 1)
                    wait(dve, out_full, BANKS * (b - 1))
                    dve.tensor_copy(parts[s][:, :, 0, :], exact[:, :, :]).then_inc(high_ready, 1)
                    dve.wait_ge(high_ready, b + 1)
                    dve.tensor_tensor(parts[s][:, :, 1, :], exact[:, :, :], parts[s][:, :, 0, :].bitcast(F32),
                                      ALU.subtract).then_inc(rest_ready, 1)

                def divide(b, k):
                    nodes = bank_tiles(k)
                    dve.wait_ge(rest_copied, BANKS * b + k + 1)
                    dve.tensor_tensor(sums[:, nodes, :], out_part(k, 0), rest_sums[:, nodes, :], ALU.add)\
                       .then_inc(sums_ready, 1)
                    dve.wait_ge(sums_ready, BANKS * b + k + 1)
                    dve.reciprocal(recip[:, nodes, :], sums[:, nodes, DIM:BOTH]).then_inc(recip_ready, 1)
                    dve.wait_ge(recip_ready, BANKS * b + k + 1)
                    wait(dve, norm.y_ready, b)
                    dve.tensor_tensor(mixed[:, nodes, :], sums[:, nodes, 0:DIM], recip[:, nodes, :], ALU.mult)\
                       .then_inc(mixed_ready, 1)

                def step(b, s):
                    if has(b + 1):
                        find_top(b + 1)
                    if has(b - 1):
                        norm.mean(dve, b)
                    if has(b + 1):
                        shift(b + 1)
                    divide(b, 0)
                    if has(b + 1):
                        split(b + 1, 1 - s)
                    divide(b, 1)
                    if has(b - 1):
                        norm.variance(dve, b)
                    if has(b + 2):
                        find_tile_top(b + 2)
                    divide(b, 2)
                    divide(b, 3)

                find_tile_top(0)
                find_top(0)
                shift(0)
                split(0, 0)
                find_tile_top(1)
                run_all(dve, step)
                norm.mean(dve, BATCH)
                norm.variance(dve, BATCH)

            @block.scalar
            def _(act):
                act.wait_ge(scale_ready, 1)

                def softplus(b, s):
                    act.activation(scaled[:, :, :], keep.x[:, b, :, :], ACT.Abs, bias=scalars[:, 1:2],
                                   scale=scalars[:, 2:3]).then_inc(scaled_ready, 1)
                    act.wait_ge(scaled_ready, b + 1)
                    wait(act, feat_ready, b - 1)
                    act.activation(decayed[:, :, :], scaled[:, :, :], ACT.Exp, scale=-1.0).then_inc(decayed_ready, 1)
                    act.activation(positive[s][:, :, :], keep.x[:, b, :, :], ACT.Relu, bias=scalars[:, 1:2],
                                   scale=scalars[:, 2:3]).then_inc(positive_ready, 1)
                    act.wait_ge(decayed_ready, b + 1)
                    act.activation(soft[s][:, :, :], decayed[:, :, :], ACT.Ln, bias=1.0).then_inc(soft_ready, 1)

                def exp(b):
                    act.wait_ge(shifted_ready, b + 1)
                    wait(act, rest_ready, b)
                    act.activation(exact[:, :, DIM:BOTH], shifted[:, :, :], ACT.Exp).then_inc(exp_ready, 1)

                def copy_totals(b):
                    act.wait_ge(total_full, b + 1)
                    wait(act, out_full, BANKS * b)
                    act.activation(totals[:, 0:DIM], ps_total[0:1, 0:DIM], ACT.Copy).then_inc(totals_ready, 1)

                def copy_rest(b, k):
                    act.wait_ge(out_full, BANKS * b + k + 1)
                    wait(act, sums_ready, BANKS * (b - 1) + k + 1)
                    act.activation(rest_sums[:, bank_tiles(k), :], out_part(k, 1), ACT.Copy).then_inc(rest_copied, 1)

                def step(b, s):
                    if has(b + 2):
                        softplus(b + 2, s)
                    copy_rest(b, 0)
                    if has(b + 1):
                        exp(b + 1)
                    copy_rest(b, 1)
                    if has(b - 1):
                        norm.square(act, b)
                    copy_rest(b, 2)
                    copy_rest(b, 3)
                    if has(b + 1):
                        copy_totals(b + 1)

                softplus(0, 0)
                exp(0)
                copy_totals(0)
                softplus(1, 1)
                run_all(act, step)
                norm.square(act, BATCH)

            @block.tensor
            def _(pe):

                def turn_top(b):
                    pe.wait_ge(tile_top_ready, b + 1)
                    wait(pe, top_ready, b)
                    pe.matmul(ps_top[0:DIM, 0:P], tile_top[:, :], keep.ident[:, :], start=True, stop=True)\
                      .then_inc(top_full, 1)

                def spread_top(b):
                    pe.wait_ge(diag_ready, b + 1)
                    wait(pe, shifted_ready, b)
                    pe.matmul(ps_wide[:, 0:DIM], keep.ones[0:DIM, :], top_diag[:, :], start=True, stop=True)\
                      .then_inc(wide_full, 1)

                def sum_up(b, s):
                    pe.wait_ge(feat_ready, b + 1)
                    wait(pe, totals_ready, b + 1)
                    for t in range(TILES):
                        last = pe.matmul(ps_total[0:1, 0:DIM], keep.ones[:, 0:1], feat[s][:, t, :],
                                         start=(t == 0), stop=(t == TILES - 1))
                    last.then_inc(total_full, 1)

                def multiply(b, s, k):
                    if k == 0:
                        pe.wait_ge(rest_ready, b + 1)
                        pe.wait_ge(totals_ready, b + 2)
                    wait(pe, sums_ready, BANKS * (b - 1) + k + 1)
                    for n in range(BANK_TILES):
                        i = k * BANK_TILES + n
                        out = ps_out[k][:, 2 * n * BOTH:2 * (n + 1) * BOTH]
                        for t in range(TILES):
                            pe.matmul(out, keep.mask[:, t, i * P:(i + 1) * P],
                                      parts[s][:, t, :, :].rearrange("p s c -> p (s c)"), start=(t == 0), stop=False,
                                      skip_group_check=True)
                        last = pe.matmul(out[:, 0:BOTH], keep.empty[:, i * P:(i + 1) * P], totals[:, :],
                                         start=False, stop=True, skip_group_check=True)
                    last.then_inc(out_full, 1)

                def step(b, s):
                    if has(b + 1):
                        turn_top(b + 1)
                    multiply(b, s, 0)
                    if has(b + 1):
                        spread_top(b + 1)
                    multiply(b, s, 1)
                    multiply(b, s, 2)
                    multiply(b, s, 3)
                    if has(b + 1):
                        sum_up(b + 1, 1 - s)

                turn_top(0)
                spread_top(0)
                sum_up(0, 0)
                run_all(pe, step)




class Keep:

    def __init__(self, mem):
        self.x = mem.sbuf("x", [P, BATCH + 1, TILES, DIM])
        self.first_x_loaded = mem.semaphore("first_x_loaded")
        self.x_loaded = mem.semaphore("x_loaded")
        self.mask = mem.sbuf("mask", [P, TILES, NODES], F32R)
        self.empty = mem.sbuf("empty", [1, NODES])
        self.no_neighbour = mem.sbuf("no_neighbour", [P, TILES])
        self.ident = mem.sbuf("ident", [P, P])
        self.ones = mem.sbuf("ones", [P, P])
        self.minus_half = mem.sbuf("minus_half", [P, TILES])


def build(nc, ins, out):
    with ExitStack() as stack:
        keep = Keep(Memory(nc, stack, "keep"))
        setup(nc, ins, keep)
        additive_layer(nc, "first", keep, ins["L0_gnn_W"], ins["L0_gnn_a"], x_rows(ins))
        feature_layer(nc, "second", keep, ins)
        additive_layer(nc, "third", keep, ins["L2_gnn_W"], ins["L2_gnn_a"])
        dot_layer(nc, "fourth", keep, ins, out)


INPUTS = ["x", "adj", "L0_gnn_W", "L0_gnn_a", "L1_gnn_w0", "L1_gnn_b0", "L1_gnn_wa", "L1_gnn_ba", "L2_gnn_W",
          "L2_gnn_a", "L3_gnn_Wh", "L3_gnn_bh", "L3_gnn_Wo", "L3_gnn_bo", "L3_gnn_gamma", "L3_gnn_beta"]


def kernel(**inputs):
    import numpy as np
    import concourse.bacc as bacc
    from concourse.bass_utils import run_bass_kernel_spmd

    nc = bacc.Bacc("TRN2", target_bir_lowering=False, num_devices=1)
    arrays, ins = {}, {}
    for name in INPUTS:
        a = np.ascontiguousarray(inputs[name])
        arrays[f"in_{name}"] = a
        ins[name] = nc.dram_tensor(f"in_{name}", a.shape, mybir.dt.from_np(a.dtype), kind="ExternalInput").ap()
    out = nc.dram_tensor("out", (BATCH, NODES, DIM), F32, kind="ExternalOutput").ap()
    build(nc, ins, out)
    result = run_bass_kernel_spmd(nc, [arrays], core_ids=[0])
    return result.results[0]["out"]
```
